# Optimizing a Trainium2 kernel written in Bass

```python
import numpy as np
import jax
import jax.numpy as jnp

def _softmax(x, axis=-1):
    return jax.nn.softmax(x, axis=axis)

def _gelu(x):
    return jax.nn.gelu(x, approximate=True)

def _silu(x):
    return jax.nn.silu(x)

def _sigmoid(x):
    return jax.nn.sigmoid(x)

def _layernorm(x, axis=-1, eps=1e-05):
    m = jnp.mean(x, axis=axis, keepdims=True)
    v = jnp.var(x, axis=axis, keepdims=True)
    return (x - m) / jnp.sqrt(v + eps)

def _scatter_add(tgt, idx, src, axis=0):
    return tgt.at[idx].add(src)

def _segment_sum(src, seg, n):
    return jax.ops.segment_sum(src, seg, n)
kernel_name = 'mk_decoder_preln_d1_seqx_r4_df42ec'

def setup_inputs(seed: int=0):
    np.random.seed(seed)
    _w = jnp.asarray

    def _rec_inputs():
        import jax
        import jax.numpy as jnp
        _rk = jax.random.key(seed)
        x = -0.0005207 + 1.001 * jax.random.normal(jax.random.fold_in(_rk, 1), (32, 128, 256), jnp.float32)
        _lenS = 128 - jax.random.randint(jax.random.fold_in(_rk, 7), (32,), 0, max(1, 128 // 4) + 1, jnp.int32)
        _lenS2 = 128 - jax.random.randint(jax.random.fold_in(_rk, 8), (32,), 0, max(1, 128 // 4) + 1, jnp.int32)
        _ctx_1024P = jax.random.normal(jax.random.fold_in(_rk, 11), (32, 16, 256), jnp.float32)
        _ctx_1024c = jax.random.dirichlet(jax.random.fold_in(_rk, 511), 0.3 * jnp.ones((16,), jnp.float32), (32, 128))
        _ctx_1024t = jnp.einsum('bsk,bkd->bsd', _ctx_1024c, _ctx_1024P)
        _ctx_1024t = _ctx_1024t * jax.lax.rsqrt(jnp.mean(jnp.square(_ctx_1024t)) + 1e-12) * 0.953939
        ctx_1024 = -0.000514642 + 1.00011 * (_ctx_1024t + 0.3 * jax.random.normal(jax.random.fold_in(_rk, 611), (32, 128, 256), jnp.float32))
        return (x, ctx_1024)
    x, ctx_1024 = _rec_inputs()

    def _L0_attn_setup():
        import jax, jax.numpy as jnp
        import numpy as np
        HEADS = 16

        def _split_heads(t, h):
            b, y, hd = t.shape
            d = hd // h
            return t.reshape(b, y, h, d).transpose(0, 2, 1, 3).reshape(b * h, y, d)

        def _merge_heads(t, b, h):
            bh, y, d = t.shape
            return t.reshape(b, h, y, d).transpose(0, 2, 1, 3).reshape(b, y, h * d)
        key = jax.random.key(seed)
        ks = jax.random.split(key, 5)
        B, S, D = (8, 1024, 256)
        scale = 1.0 / np.sqrt(D)
        x = jax.random.normal(ks[0], (B, S, D), dtype=jnp.float32)
        Wq = jax.random.normal(ks[1], (D, D), dtype=jnp.float32) * scale
        Wk = jax.random.normal(ks[2], (D, D), dtype=jnp.float32) * scale
        Wv = jax.random.normal(ks[3], (D, D), dtype=jnp.float32) * scale
        Wo = jax.random.normal(ks[4], (D, D), dtype=jnp.float32) * scale
        return {'x': x, 'Wq': Wq, 'Wk': Wk, 'Wv': Wv, 'Wo': Wo}
    _L0_attn_all = _L0_attn_setup()
    _L0_attn_in = {k: v for k, v in _L0_attn_all.items() if k in ('Wq', 'Wk', 'Wv', 'Wo')}
    del _L0_attn_all

    def _L0_xattn_setup():
        import jax, jax.numpy as jnp
        import numpy as np
        DIM = 256
        HEADS = 8
        HEAD_DIM = DIM // HEADS
        TAU = HEAD_DIM ** 0.5
        BS, SEQ = (1, 512)
        key = jax.random.key(seed)
        kq, kk, kv, kb = jax.random.split(key, 4)
        q = jax.random.normal(kq, (BS, SEQ, DIM), jnp.float32)
        k = jax.random.normal(kk, (BS, SEQ, DIM), jnp.float32)
        v = jax.random.normal(kv, (BS, SEQ, DIM), jnp.float32)
        Wi_w = jnp.zeros((HEADS, 3 * DIM), jnp.float32)
        Wi_b = 0.1 * jax.random.normal(kb, (HEADS,), jnp.float32)
        Wf_w = jnp.zeros((HEADS, 3 * DIM), jnp.float32)
        Wf_b = jnp.linspace(3.0, 6.0, HEADS, dtype=jnp.float32)
        gn_w = jnp.ones((DIM,), jnp.float32)
        gn_b = jnp.zeros((DIM,), jnp.float32)
        return {'q': q, 'k': k, 'v': v, 'Wi_w': Wi_w, 'Wi_b': Wi_b, 'Wf_w': Wf_w, 'Wf_b': Wf_b, 'gn_w': gn_w, 'gn_b': gn_b}
    _L0_xattn_all = _L0_xattn_setup()
    _L0_xattn_in = {k: v for k, v in _L0_xattn_all.items() if k in ('Wi_w', 'Wi_b', 'Wf_w', 'Wf_b', 'gn_w', 'gn_b')}
    del _L0_xattn_all

    def _L0_ffn_setup():
        import jax, jax.numpy as jnp
        import numpy as np
        E = 16
        K = 4
        B, S, H, I = (4, 256, 256, 512)
        key = jax.random.key(seed)
        k0, k1, k2, k3 = jax.random.split(key, 4)
        scale = 0.02
        return {'hidden_states': jax.random.normal(k0, (B, S, H), jnp.float32), 'router_w': jax.random.normal(k1, (H, E), jnp.float32) * scale, 'router_b': jnp.zeros((E,), jnp.float32), 'w1': jax.random.normal(k2, (E, H, I), jnp.float32) * scale, 'b1': jnp.zeros((E, I), jnp.float32), 'w2': jax.random.normal(k3, (E, I, H), jnp.float32) * scale, 'b2': jnp.zeros((E, H), jnp.float32)}
    _L0_ffn_all = _L0_ffn_setup()
    _L0_ffn_in = {k: v for k, v in _L0_ffn_all.items() if k in ('router_w', 'router_b', 'w1', 'b1', 'w2', 'b2')}
    del _L0_ffn_all
    return {'x': x, 'ctx_1024': ctx_1024, 'L0_attn_Wq': _L0_attn_in['Wq'], 'L0_attn_Wk': _L0_attn_in['Wk'], 'L0_attn_Wv': _L0_attn_in['Wv'], 'L0_attn_Wo': _L0_attn_in['Wo'], 'L0_xattn_Wi_w': _L0_xattn_in['Wi_w'], 'L0_xattn_Wi_b': _L0_xattn_in['Wi_b'], 'L0_xattn_Wf_w': _L0_xattn_in['Wf_w'], 'L0_xattn_Wf_b': _L0_xattn_in['Wf_b'], 'L0_xattn_gn_w': _L0_xattn_in['gn_w'], 'L0_xattn_gn_b': _L0_xattn_in['gn_b'], 'L0_ffn_router_w': _L0_ffn_in['router_w'], 'L0_ffn_router_b': _L0_ffn_in['router_b'], 'L0_ffn_w1': _L0_ffn_in['w1'], 'L0_ffn_b1': _L0_ffn_in['b1'], 'L0_ffn_w2': _L0_ffn_in['w2'], 'L0_ffn_b2': _L0_ffn_in['b2']}

def reference(x, ctx_1024, L0_attn_Wq, L0_attn_Wk, L0_attn_Wv, L0_attn_Wo, L0_xattn_Wi_w, L0_xattn_Wi_b, L0_xattn_Wf_w, L0_xattn_Wf_b, L0_xattn_gn_w, L0_xattn_gn_b, L0_ffn_router_w, L0_ffn_router_b, L0_ffn_w1, L0_ffn_b1, L0_ffn_w2, L0_ffn_b2):
    import jax
    import jax.numpy as jnp

    def _L0_attn_ref(x, Wq, Wk, Wv, Wo):
        import jax, jax.numpy as jnp
        import numpy as np
        HEADS = 16

        def _split_heads(t, h):
            b, y, hd = t.shape
            d = hd // h
            return t.reshape(b, y, h, d).transpose(0, 2, 1, 3).reshape(b * h, y, d)

        def _merge_heads(t, b, h):
            bh, y, d = t.shape
            return t.reshape(b, h, y, d).transpose(0, 2, 1, 3).reshape(b, y, h * d)
        b = x.shape[0]
        h = HEADS
        q = _split_heads(x @ Wq.T, h)
        k = _split_heads(x @ Wk.T, h)
        v = _split_heads(x @ Wv.T, h)
        d = q.shape[-1]
        z = jnp.einsum('byq,byk->bkq', q, k) / jnp.sqrt(jnp.asarray(d, x.dtype))
        z = jax.nn.softmax(z, axis=-1)
        z = jnp.einsum('byz,bvy->bvz', z, v)
        z = _merge_heads(z, b, h)
        return z @ Wo.T

    def _L0_xattn_ref(q, k, v, Wi_w, Wi_b, Wf_w, Wf_b, gn_w, gn_b):
        import jax, jax.numpy as jnp
        import numpy as np
        DIM = 256
        HEADS = 8
        HEAD_DIM = DIM // HEADS
        TAU = HEAD_DIM ** 0.5
        BS, SEQ = (1, 512)
        bs, seq, dim = q.shape
        gate_in = jnp.concatenate([q, k, v], axis=-1)
        itilde = jnp.einsum('bsd,hd->bhs', gate_in, Wi_w) + Wi_b[None, :, None]
        ftilde = jnp.einsum('bsd,hd->bhs', gate_in, Wf_w) + Wf_b[None, :, None]
        csum = jnp.cumsum(jax.nn.log_sigmoid(ftilde), axis=-1)
        Fmat = csum[..., :, None] - csum[..., None, :]
        mask = jnp.tril(jnp.ones((seq, seq), dtype=bool))
        F_act = jnp.where(mask, Fmat, -jnp.inf)
        Dtilde = F_act + itilde[..., None, :]
        max_d = jnp.max(Dtilde, axis=-1, keepdims=True)
        D = jnp.exp(Dtilde - max_d)
        qh = q.reshape(bs, seq, HEADS, HEAD_DIM).transpose(0, 2, 1, 3)
        kh = k.reshape(bs, seq, HEADS, HEAD_DIM).transpose(0, 2, 1, 3)
        vh = v.reshape(bs, seq, HEADS, HEAD_DIM).transpose(0, 2, 1, 3)
        Ctilde = jnp.einsum('bhid,bhjd->bhij', qh, kh) * D / TAU
        maxit = jnp.maximum(jnp.abs(jnp.sum(Ctilde, axis=-1, keepdims=True)), jnp.exp(-max_d))
        Htilde = jnp.einsum('bhij,bhjd->bhid', Ctilde, vh) / (maxit + 1e-06)
        x = Htilde.transpose(0, 2, 1, 3).reshape(bs * seq, HEADS, HEAD_DIM)
        mean = jnp.mean(x, axis=-1, keepdims=True)
        var = jnp.var(x, axis=-1, keepdims=True)
        xn = (x - mean) / jnp.sqrt(var + 1e-05)
        out = xn.reshape(bs * seq, DIM) * gn_w + gn_b
        return out.reshape(bs, seq, DIM)

    def _L0_ffn_ref(hidden_states, router_w, router_b, w1, b1, w2, b2):
        import jax, jax.numpy as jnp
        import numpy as np
        E = 16
        K = 4
        B, S, H, I = (4, 256, 256, 512)
        b, s, h = hidden_states.shape
        logits = hidden_states @ router_w + router_b
        probs = jax.nn.softmax(logits, axis=-1)
        topw, topi = jax.lax.top_k(probs, K)
        topw = topw / jnp.sum(topw, axis=-1, keepdims=True)
        combine = jnp.sum(jax.nn.one_hot(topi, E, dtype=hidden_states.dtype) * topw[..., None], axis=2)
        x = hidden_states.reshape(b * s, h)
        c = combine.reshape(b * s, E)

        def body(acc, expert):
            w1e, b1e, w2e, b2e, ce = expert
            hmid = jax.nn.gelu(x @ w1e + b1e, approximate=False)
            return (acc + (hmid @ w2e + b2e) * ce[:, None], None)
        out, _ = jax.lax.scan(body, jnp.zeros_like(x), (w1, b1, w2, b2, c.T))
        return out.reshape(b, s, h)
    x = x + _L0_attn_ref(_layernorm(x, axis=-1), L0_attn_Wq, L0_attn_Wk, L0_attn_Wv, L0_attn_Wo)
    x = x + _L0_xattn_ref(_layernorm(x, axis=-1), ctx_1024, ctx_1024, L0_xattn_Wi_w, L0_xattn_Wi_b, L0_xattn_Wf_w, L0_xattn_Wf_b, L0_xattn_gn_w, L0_xattn_gn_b)
    x = x + _L0_ffn_ref(_layernorm(x, axis=-1), L0_ffn_router_w, L0_ffn_router_b, L0_ffn_w1, L0_ffn_b1, L0_ffn_w2, L0_ffn_b2)
    return x

_drawn_inputs = setup_inputs


def setup_inputs(seed=0):
    import zlib

    import numpy as np

    out = dict(_drawn_inputs(seed))
    spreads = {'L0_xattn_Wi_w': (0.0, 0.1),
     'L0_xattn_Wf_w': (0.0, 0.1),
     'L0_xattn_gn_w': (1.0, 0.2),
     'L0_xattn_gn_b': (0.0, 0.1),
     'L0_ffn_router_b': (0.0, 0.445),
     'L0_ffn_b1': (0.0, 0.8),
     'L0_ffn_b2': (0.0, 0.283)}
    factors = {'L0_xattn_Wi_b': 64.0}
    for name, (base, spread) in spreads.items():
        noise = np.random.default_rng([zlib.crc32(name.encode()), seed]).standard_normal(out[name].shape)
        drawn = base * np.exp(spread * noise) if base else spread * noise
        out[name] = jnp.asarray(drawn.astype(out[name].dtype))
    for name, factor in factors.items():
        out[name] = (out[name] * factor).astype(out[name].dtype)
    return out
```

```python
import concourse.bass as bass
import concourse.mybir as mybir
import numpy as np
from contextlib import ExitStack

F32 = mybir.dt.float32
F32R = mybir.dt.float32r
BF16 = mybir.dt.bfloat16
U32 = mybir.dt.uint32
I32 = mybir.dt.int32
ALU = mybir.AluOpType
ACT = mybir.ActivationFunctionType
AX = mybir.AxisListType

P = 128
SEQS, LEN, DIM = 32, 128, 256
CH = DIM // P
A_HEADS, X_HEADS = 16, 8
A_DH, X_DH = DIM // A_HEADS, DIM // X_HEADS
TOKENS = SEQS * LEN
EXPERTS, TOP_K, HID = 16, 4, 512
HC = HID // P
EPS = 1e-5
TAU = X_DH ** 0.5
MASKED = -1e30

ROWS = 256
BLOCKS = ROWS // P
REGION = TOKENS + ROWS
C_ROW = DIM + EXPERTS
PAY = C_ROW + 16
MAX_TILES = TOKENS * TOP_K // ROWS + EXPERTS
OUT_ROWS = TOKENS + ROWS
CROSS_LAGS = 8
NORMS = 2 + X_HEADS
GROUPS = X_DH + 1

C_ID, C_TRI, C_CAUSAL, C_BLOCK, C_TRIX, C_CENTRE, C_IOTA, C_BASE, C_THR, C_PADROW, C_END = (
    0, 128, 256, 384, 512, 640, 768, 784, 800, 800 + 256, 800 + 256 + 2)
HL_ROWS = 104


def shape_constants():
    c = np.zeros((P, C_END), np.float32)
    p, q = np.arange(P)[:, None], np.arange(P)[None, :]
    c[:, C_ID:C_ID + P] = p == q
    c[:, C_TRI:C_TRI + P] = p <= q
    c[:, C_CAUSAL:C_CAUSAL + P] = np.where(p <= q, 0.0, MASKED)
    c[:, C_BLOCK:C_BLOCK + P] = np.where(p // A_DH == q // A_DH, 0.0, MASKED)
    c[:, C_TRIX:C_TRIX + P] = p < q
    c[:, C_CENTRE:C_CENTRE + P] = (p == q) - np.where(p // X_DH == q // X_DH, 1.0 / X_DH, 0.0)
    c[:, C_IOTA:C_IOTA + EXPERTS] = np.arange(EXPERTS)
    c[:, C_BASE:C_BASE + EXPERTS] = np.arange(EXPERTS) * REGION
    c[:, C_THR:C_THR + 256] = np.tile(ROWS * np.r_[np.arange(1, 16), 10 ** 9], EXPERTS)
    c[:, C_PADROW:C_PADROW + BLOCKS] = p + P * np.arange(BLOCKS)[None, :]
    s = np.zeros((HL_ROWS, 2 * X_HEADS * P), np.float32)
    minus_max = s[:, :X_HEADS * P].reshape(HL_ROWS, X_HEADS, P)
    plus_a = s[:, X_HEADS * P:2 * X_HEADS * P].reshape(HL_ROWS, X_HEADS, P)
    for h in range(X_HEADS):
        plus_a[[h, 64 + h], h] = 1.0
        minus_max[[32 + h, 96 + h], h] = -1.0
    rows = np.arange(SEQS + BLOCKS, dtype=np.int32)[None, :] * P + np.arange(P, dtype=np.int32)[:, None]
    return c, s, rows


class Step:

    def __init__(self, sem, n=1):
        self.sem, self.n = sem, n

    def at(self, t, j=None):
        return self.n * t + (self.n if j is None else j)


def has(t):
    return not (isinstance(t, int) and t < 0)


def skewed(engine, items, lags, body):
    def peeled(i):
        body(i, i % 2, lambda lag: 0 <= i - lag < items, lambda lag: (i - lag) // 2)

    first, last = lags + 2 - lags % 2, items - items % 2
    for i in range(first):
        peeled(i)
    with engine.Fori(first // 2, last // 2) as k:
        for u in range(2):
            body(2 * k + u, u, lambda lag: True, lambda lag: k + (u - lag) // 2)
    for i in range(last, items + lags):
        peeled(i)


def decoder_layer(nc, x, ctx_t, w_qk_t, w_v_t, w_o_t, gate_w_t, gate_b, gn_w, gn_b,
                  router_w, router_b, w1, b1, w2, b2, consts, selectors, row_ids, out):
    stack = ExitStack()
    with stack:
        def sb(name, shape, dt=F32):
            return stack.enter_context(nc.sbuf_tensor(name, shape, dt))

        def step(name, n=1):
            return Step(stack.enter_context(nc.semaphore(name)), n)

        psum = stack.enter_context(nc.psum_tensor("psum", [P, 8, 512], F32))
        banks = [psum[:, i, :] for i in range(8)]

        routed = nc.dram_tensor("routed_rows", [EXPERTS * REGION, PAY], F32, kind="Internal").ap()

        cst = sb("cst", [P, C_END])
        ident = cst[:, C_ID:C_ID + P]
        tri = cst[:, C_TRI:C_TRI + P]
        block_mask = cst[:, C_BLOCK:C_BLOCK + P]
        centre = cst[:, C_CENTRE:C_CENTRE + P]
        iota16 = cst[:, C_IOTA:C_IOTA + EXPERTS]
        sel_in = sb("sel_in", [HL_ROWS, 2 * X_HEADS * P])
        sel_r = sb("sel_r", [HL_ROWS, 2 * X_HEADS * P], F32R)
        sel_max = sel_r[:, 0:X_HEADS * P].rearrange("k (h j) -> k h j", h=X_HEADS)
        sel_a = sel_r[:, X_HEADS * P:2 * X_HEADS * P]
        ident_r = sb("ident_r", [P, P], F32R)
        causal_r = sb("causal_r", [P, 4, P], F32R)
        tri_before = sb("tri_before", [P, P], BF16)
        ones_bf = sb("ones_bf", [P, P], BF16)
        half = sb("half", [P, X_HEADS])
        eps = sb("eps", [P, X_HEADS])
        gate_bias = sb("gate_bias", [40, 1])
        minus_bias = sb("minus_bias", [X_HEADS, 1])
        gnw = sb("gnw", [P, DIM])
        gnb = sb("gnb", [P, DIM])
        rbias = sb("rbias", [P, EXPERTS])
        rw = sb("rw", [P, CH, EXPERTS])
        b2_sb = sb("b2_sb", [EXPERTS, DIM])
        b1_sb = sb("b1_sb", [P, EXPERTS, HC])
        gw = sb("gw", [P, 3 * CH, 2 * X_HEADS])
        gw_t = sb("gw_t", [P, 2 * CH, 40])


        wqk = sb("wqk", [P, CH, 2 * DIM])
        wv = sb("wv", [P, CH, DIM])
        wo = sb("wo", [P, CH, DIM])
        a_stat = sb("a_stat", [P, 2, 6])
        a_mv = sb("a_mv", [P, 2, 2])
        a_var = sb("a_var", [P, 2])
        a_rstd = sb("a_rstd", [P, 2])
        a_xn = sb("a_xn", [P, 2, DIM])
        a_xnt = sb("a_xnt", [P, CH, 2, P])
        a_qk = sb("a_qk", [P, 2, 2 * DIM])
        a_vt = sb("a_vt", [P, 2, CH, 2, P])
        a_z = sb("a_z", [P, 4, P])
        a_p = sb("a_p", [P, 4, P])
        a_pn = sb("a_pn", [P, 4, P])
        a_max = sb("a_max", [P, 4])
        a_neg = sb("a_neg", [P, 4])
        a_sum = sb("a_sum", [P, 4])
        a_inv = sb("a_inv", [P, 4])
        a_z2 = sb("a_z2", [P, CH, 2, P])
        ps_t, ps_qk, ps_av, ps_z, ps_z2, ps_o = banks[0], banks[1:3], banks[3], banks[4], banks[5], banks[6]

        ld_cst = step("ld_cst", 16)
        ld_sel = step("ld_sel", 16)
        ld_x = [step(f"ld_x{u}", 16) for u in range(2)]
        ld_wa = step("ld_wa", 48)
        ld_small = step("ld_small", 16 * 10)
        ld_b1 = step("ld_b1", 16)
        cst_ready = step("cst_ready", 2)

        a_stats = step("a_stats", 4)
        a_norm = step("a_norm", 2)
        a_ready = step("a_ready", 2)
        a_t = step("a_t")
        a_tc = step("a_tc")
        a_proj = step("a_proj", 2)
        a_projc = step("a_projc", 2)
        a_v = step("a_v")
        a_vc = step("a_vc")
        a_zz = step("a_zz")
        a_zm = step("a_zm", 3)
        a_e = step("a_e", 4)
        a_sc = step("a_sc", 2)
        a_pv = step("a_pv")
        a_pvc = step("a_pvc")
        a_o = step("a_o")
        a_res = step("a_res")
        PAIRS = SEQS // 2

        n_stat = sb("n_stat", [P, 2, 6])
        n_mv = sb("n_mv", [P, 2, 2])
        n_var = sb("n_var", [P, NORMS])
        n_rstd = sb("n_rstd", [P, NORMS])
        n_half = sb("n_half", [P, NORMS])
        n_mr = sb("n_mr", [P, 2])
        x_q = sb("x_q", [P, DIM])
        h_abs = sb("h_abs", [P, X_HEADS])
        h_e2 = sb("h_e2", [P, X_HEADS])
        h_fw = sb("h_fw", [P, DIM])
        c_t = sb("c_t", [P, 2, CH, P])
        c_x = sb("c_x", [P, 2, CH, 4, P])
        v_c = sb("v_c", [P, 2, X_HEADS, GROUPS])
        x_qt = sb("x_qt", [P, 2, CH, P])
        x_abs = sb("x_abs", [X_HEADS, P])
        x_relu = sb("x_relu", [X_HEADS, P])
        x_ncs = sb("x_ncs", [40, P])
        x_m = sb("x_m", [40, 2, P])
        x_ea = sb("x_ea", [X_HEADS, P])
        x_ln = sb("x_ln", [X_HEADS, P])
        x_am = sb("x_am", [40, P])
        x_hl = sb("x_hl", [HL_ROWS, 2, P], F32R)
        x_d = sb("x_d", [P, X_HEADS, P])
        x_c = sb("x_c", [P, X_HEADS, P])
        x_em = sb("x_em", [P, X_HEADS])
        h_sq = sb("h_sq", [P, X_HEADS, X_DH])
        h_max = sb("h_max", [P, X_HEADS])
        h_den = sb("h_den", [P, X_HEADS])
        h_ss = sb("h_ss", [P, X_HEADS])
        h_n = sb("h_n", [P, DIM])
        pay = sb("pay", [P, 2, PAY])
        r_xt = sb("r_xt", [P, CH, P])
        r_lg = sb("r_lg", [P, EXPERTS])
        r_top = sb("r_top", [P, 8])
        r_idx = sb("r_idx", [P, 8], U32)
        r_neg = sb("r_neg", [P, 1])
        r_e = sb("r_e", [P, EXPERTS])
        r_hot = sb("r_hot", [P, TOP_K, EXPERTS])
        r_maskb = sb("r_maskb", [P, EXPERTS], BF16)
        r_me = sb("r_me", [P, EXPERTS])
        r_s = sb("r_s", [P, 1])
        r_i = sb("r_i", [P, 1])
        r_base = sb("r_base", [P, EXPERTS])
        r_pos = sb("r_pos", [P, EXPERTS])
        r_dsel = sb("r_dsel", [P, TOP_K, EXPERTS])
        r_dstf = sb("r_dstf", [P, TOP_K])
        r_dst = sb("r_dst", [P, 2, TOP_K], U32)
        r_ct = sb("r_ct", [EXPERTS, P])
        o_init = sb("o_init", [P, 2, DIM])
        rows_id = sb("rows_id", [P, SEQS + BLOCKS], I32)
        pad = sb("pad", [P, BLOCKS, PAY])
        t_ones = sb("t_ones", [P, EXPERTS])
        t_cnt = sb("t_cnt", [P, EXPERTS])
        t_cmp = sb("t_cmp", [P, EXPERTS, 16])
        t_num = sb("t_num", [P, EXPERTS])
        t_scan = sb("t_scan", [P, EXPERTS + 1])
        t_first = sb("t_first", [P, EXPERTS + 1], I32)
        t_end = sb("t_end", [P, EXPERTS], I32)

        ps_s = psum[:, 0:2, :].rearrange("p k (h i) -> p (k h) i", h=4)
        ps_arg = banks[2:4]
        ps_qt = banks[4][:, 0:256].rearrange("p (c i) -> p c i", c=CH)
        ps_xt = banks[4][:, 256:512].rearrange("p (c i) -> p c i", c=CH)
        ps_v = banks[4][:, 0:256]
        ps_init = banks[4][:, 256:512]
        ps_h = [banks[5 + u][:, 0:X_HEADS * GROUPS].rearrange("p (h d) -> p h d", h=X_HEADS) for u in range(2)]
        ps_mt = [banks[5 + u][:, 288:296] for u in range(2)]
        ps_lg, ps_pos, ps_tot = (banks[7][:, 16 * k:16 * k + 16] for k in range(3))
        ps_f = banks[7][0:X_HEADS, 128:256]
        ps_i = banks[7][32:32 + X_HEADS, 128:256]
        ps_gates = banks[7][0:40, 128:256]
        ps_ct = banks[7][0:EXPERTS, 256:384]

        ld_ct = [step(f"ld_ct{u}", 16) for u in range(2)]
        ld_cx = [step(f"ld_cx{u}", 64) for u in range(2)]
        setup = step("setup", 8)
        variances = step("variances")
        rsqrt = step("rsqrt")
        mean_r = step("mean_r")
        ln2_q = step("ln2_q")
        q_t = step("q_t")
        q_tc = step("q_tc")
        v_mm = step("v_mm")
        v_tc = step("v_tc")
        gates = step("gates")
        gates_ln = step("gates_ln")
        a_read = step("a_read")
        a_run = step("a_run")
        row_max = step("row_max")
        ncs = step("ncs")
        a_high = step("a_high")
        a_scan = step("a_scan")
        scores = step("scores")
        maxt = step("maxt")
        expm = step("expm")
        h_square = step("h_square")
        heads = step("heads")
        h_factor = step("h_factor")
        h_scale = step("h_scale")
        bias_in = step("bias_in")
        h_out = step("h_out")
        ln3_x = step("ln3_x")
        rx_t = step("rx_t")
        rx_tc = step("rx_tc")
        logits = step("logits")
        logits_b = step("logits_b")
        pick4 = step("pick4")
        rexp = step("rexp")
        weights = step("weights")
        masks = step("masks")
        place = step("place")
        placed = step("placed")
        dest = step("dest")
        w_t = step("w_t")
        w_tc = step("w_tc")
        init_mm = step("init_mm")
        init_add = step("init_add")
        args = step("args", 2)
        decay = step("decay", 2)
        weigh = step("weigh", 2)
        scatter = [step(f"scatter{u}", 16 * TOP_K) for u in range(2)]
        store = [step(f"store{u}", 16) for u in range(2)]
        trash_dma = step("trash_dma", 16)
        tiling = step("tiling")
        tail = step("tail", 16)

        w_in = sb("w_in", [P, 2, CH * HID + HC * DIM])
        W1N = CH * HID
        WN = CH * HID + HC * DIM
        parts = [sb(f"w_parts{k}", [P, WN], F32R)[:] for k in range(4)]
        xt_rows = sb("xt_rows", [P, BLOCKS, PAY])
        e_wt = sb("e_wt", [P, 2, BLOCKS, EXPERTS])
        e_id = sb("e_id", [P, 2, BLOCKS], U32)
        e_xh = sb("e_xh", [P, CH, ROWS], F32R)
        e_xl = sb("e_xl", [P, CH, ROWS], F32R)
        e_b1 = sb("e_b1", [P, HC])
        e_h = sb("e_h", [P, HC, ROWS])
        e_hh = sb("e_hh", [P, HC, ROWS], F32R)
        e_hl = sb("e_hl", [P, HC, ROWS], F32R)
        e_y = [sb(f"e_y{k}", [P, DIM]) for k in range(BLOCKS)]
        e_idx = sb("e_idx", [P, BLOCKS], U32)
        with nc.sbuf_tensor("res", [P, SEQS, DIM], F32) as res:
            pass
        parts += [sb(f"w_parts{k}", [P, WN], F32R)[:] for k in range(4, 8)]
        w_hi, w_lo = parts[0::2], parts[1::2]
        ps_hid = [banks[m][:, 0:ROWS] for m in range(HC)]
        ps_y = [banks[HC + k][:, 0:DIM] for k in range(BLOCKS)]
        ps_x = banks[HC + BLOCKS].rearrange("p (c r) -> p c r", c=CH)

        ld_w = [step(f"ld_w{u}", 32) for u in range(2)]
        w_hi_s = step("w_hi_s", 4)
        w_lo_s = step("w_lo_s", 4)
        ld_rows = step("ld_rows", 16)
        rows_t = step("rows_t")
        rows_hi = step("rows_hi")
        rows_lo = step("rows_lo")
        rows_meta = step("rows_meta")
        up = [step(f"up{m}") for m in range(HC)]
        gelu = [step(f"gelu{m}") for m in range(HC)]
        h_lo = [step(f"h_lo{m}") for m in range(HC)]
        down = step("down")
        w_done = step("w_done")
        y_out = step("y_out", BLOCKS)
        idx_out = step("idx_out")
        added = step("added", 16 * BLOCKS)

        x_v = x.rearrange("b t d -> t b d")
        out_v = out[0:TOKENS, :].rearrange("(b t) d -> t b d", t=P)
        block = stack.enter_context(nc.Block())

        def tiles_of(engine, e):
            return (0 if isinstance(e, int) and e == 0 else engine.value_load(t_first[0:1, bass.ds(e, 1)], min_val=0, max_val=MAX_TILES),
                    engine.value_load(t_first[0:1, bass.ds(e + 1, 1)], min_val=1, max_val=MAX_TILES))

        def load_w(engine, e, u):
            engine.dma_start(w_in[:, u, 0:W1N].rearrange("p (c n) -> p c n", c=CH),
                             w1[bass.ds(e, 1)].rearrange("a (c p) n -> p (a c) n", p=P)).then_inc(ld_w[u].sem, 16)
            engine.dma_start(w_in[:, u, W1N:].rearrange("p (c n) -> p c n", c=HC),
                             w2[bass.ds(e, 1)].rearrange("a (c p) n -> p (a c) n", p=P)).then_inc(ld_w[u].sem, 16)

        def parity(i):
            return i % 2

        def seq(t):
            return res[:, bass.ds(t, 1), :].rearrange("p a d -> p (a d)")

        @block.sync
        def _(sp):
            sp.dma_start(cst[:], consts).then_inc(ld_cst.sem, 16)

            def load_x(p, u):
                sp.dma_start(res[:, bass.ds(2 * p, 2), :], x_v[:, bass.ds(2 * p, 2), :]).then_inc(ld_x[u].sem, 16)

            load_x(0, 0)
            load_x(1, 1)
            sp.dma_start(wqk[:], w_qk_t.rearrange("(c p) n -> p c n", p=P)).then_inc(ld_wa.sem, 16)
            sp.dma_start(wv[:], w_v_t.rearrange("(c p) n -> p c n", p=P)).then_inc(ld_wa.sem, 16)
            sp.dma_start(wo[:], w_o_t.rearrange("(c p) n -> p c n", p=P)).then_inc(ld_wa.sem, 16)
            with sp.Fori(1, PAIRS // 2) as k:
                for u in range(2):
                    if has(k - 1):
                        sp.wait_ge(ld_x[u].sem, ld_x[u].at(k - 1))
                    load_x(2 * k + u, u)
            sp.dma_start(sel_in[:], selectors).then_inc(ld_small.sem, 16)
            sp.dma_start(rows_id[:], row_ids).then_inc(ld_small.sem, 16)
            for dst, src in ((gnb, gn_b), (gnw, gn_w), (rbias, router_b)):
                sp.dma_start(dst[:], src.rearrange("(a n) -> a n", a=1).to_broadcast([P, dst.shape[1]])
                             ).then_inc(ld_small.sem, 16)
            for row, at in ((0, X_HEADS), (32, 0)):
                sp.dma_start(gate_bias[row:row + X_HEADS], gate_b[at:at + X_HEADS].rearrange("(h a) -> h a", a=1)
                             ).then_inc(ld_small.sem, 16)
            sp.dma_start(rw[:], router_w.rearrange("(c p) n -> p c n", p=P)).then_inc(ld_small.sem, 16)
            sp.dma_start(b2_sb[:], b2).then_inc(ld_small.sem, 16)
            sp.dma_start(b1_sb[:], b1).then_inc(ld_b1.sem, 16)
            sp.dma_start(gw[:], gate_w_t.rearrange("(c p) n -> p c n", p=P)).then_inc(ld_small.sem, 16)

            load_w(sp, 0, 0)
            load_w(sp, 1, 1)
            sp.wait_ge(setup.sem, setup.at(0))
            sp.dma_start(out[TOKENS:OUT_ROWS, :].rearrange("(k p) n -> p k n", p=P),
                         pad[:, :, 0:DIM]).then_inc(trash_dma.sem, 16)

            def cross(i, u, on, half_):
                if on(0):
                    if has(i - 2):
                        sp.wait_ge(gates.sem, gates.at(i - 2))
                        sp.wait_ge(scores.sem, scores.at(i - 2))
                        sp.wait_ge(v_mm.sem, v_mm.at(i - 2))
                    sp.dma_start(c_t[:, u], ctx_t[bass.ds(i, 1)].rearrange("a (c p) i -> p (a c) i", p=P)
                                 ).then_inc(ld_ct[u].sem, 16)
                    for r in range(4):
                        sp.dma_start(c_x[X_DH * r:X_DH * (r + 1), u, :, r],
                                     ctx_t[bass.ds(i, 1)].rearrange("a (c r p) i -> r p (a c) i", c=CH, r=4)[r]
                                     ).then_inc(ld_cx[u].sem, 16)
                if on(8):
                    sp.wait_ge(init_add.sem, init_add.at(i - 8))
                    sp.dma_start(out_v[:, bass.ds(i - 8, 1), :], o_init[:, u].rearrange("p (a d) -> p a d", a=1)
                                 ).then_inc(store[u].sem, 16)

            skewed(sp, SEQS, CROSS_LAGS, cross)

            for u in range(2):
                sp.wait_ge(scatter[u].sem, scatter[u].at(SEQS // 2 - 1))
            sp.wait_ge(tiling.sem, tiling.at(0))

            def write_tail(e):
                row = sp.value_load(t_end[0:1, bass.ds(e, 1)], min_val=0, max_val=(EXPERTS - 1) * REGION + TOKENS)
                if has(e - 1):
                    sp.wait_ge(tail.sem, tail.at(e - 1))
                sp.dma_start(routed[bass.ds(row, ROWS), :].rearrange("(k p) n -> p k n", p=P), pad[:]
                             ).then_inc(tail.sem, 16)

            def load_rows(i, e, row):
                sp.wait_ge(tail.sem, tail.at(e))
                if has(i - 1):
                    sp.wait_ge(rows_t.sem, rows_t.at(i - 1))
                if has(i - 1):
                    sp.wait_ge(rows_meta.sem, rows_meta.at(i - 1))
                sp.dma_start(xt_rows[:], routed[bass.ds(row, ROWS), :].rearrange("(k p) n -> p k n", p=P)
                             ).then_inc(ld_rows.sem, 16)

            def expert(e, tail_follows):
                first, end = tiles_of(sp, e)
                if tail_follows:
                    write_tail(e + 1)

                def load(i):
                    load_rows(i, e, nc.s_assert_within(
                        (i - first) * ROWS + e * REGION, 0, EXPERTS * REGION - ROWS,
                        skip_runtime_bounds_check_because="an expert's tiles lie in its region"))

                load(first)
                with sp.If(end > first + 1):
                    with sp.Fori(first + 1, end) as i:
                        load(i)

            write_tail(0)
            expert(0, True)
            with sp.Fori(1, EXPERTS - 1) as e:
                expert(e, True)
            expert(EXPERTS - 1, False)
            total = sp.value_load(t_first[0:1, EXPERTS:EXPERTS + 1], min_val=EXPERTS, max_val=MAX_TILES)
            load_rows(total, EXPERTS - 1, 0)
            sp.wait_ge(trash_dma.sem, trash_dma.at(0))
            for u in range(2):
                sp.wait_ge(store[u].sem, store[u].at(SEQS // 2 - 1))

        @block.gpsimd
        def _(pool):
            pool.memset(half[:], -0.5).then_inc(cst_ready.sem, 1)
            pool.memset(eps[:], EPS).then_inc(cst_ready.sem, 1)
            pool.wait_ge(cst_ready.sem, cst_ready.at(0))

            def attention(i, u, on, half_):
                if on(0):
                    pool.wait_ge(a_stats.sem, a_stats.at(i))
                    if has(i - 1):
                        pool.wait_ge(a_ready.sem, a_ready.at(i - 1))
                    pool.tensor_tensor(a_var[:], a_mv[:, :, 1], eps[:, 0:2], ALU.add).then_inc(a_norm.sem, 1)
                    pool.wait_ge(a_norm.sem, a_norm.at(i, 1))
                    pool.tensor_tensor(a_rstd[:], a_var[:], half[:, 0:2], ALU.pow).then_inc(a_norm.sem, 1)

            skewed(pool, PAIRS, 4, attention)
            pool.wait_ge(setup.sem, setup.at(0))

            def cross(i, u, on, half_):
                v = (u + 1) % 2
                if on(0) or on(4):
                    pool.wait_ge(variances.sem, variances.at(i))
                    if has(i - 1):
                        pool.wait_ge(mean_r.sem, mean_r.at(i - 1))
                    if on(1):
                        pool.wait_ge(ln2_q.sem, ln2_q.at(i - 1))
                    if on(5):
                        pool.wait_ge(ln3_x.sem, ln3_x.at(i - 5))
                    pool.tensor_tensor(n_rstd[:], n_var[:], n_half[:], ALU.pow).then_inc(rsqrt.sem, 1)
                if on(3):
                    pool.wait_ge(rsqrt.sem, rsqrt.at(i))
                    if has(i - 4):
                        pool.wait_ge(h_scale.sem, h_scale.at(i - 4))
                    pool.tensor_tensor(h_fw[:].rearrange("p (h d) -> p h d", d=X_DH),
                                       n_rstd[:, 2:].rearrange("p (h a) -> p h a", a=1).to_broadcast([P, X_HEADS, X_DH]),
                                       gnw[:].rearrange("p (h d) -> p h d", d=X_DH), ALU.mult).then_inc(h_factor.sem, 1)
                if on(1):
                    pool.wait_ge(ln2_q.sem, ln2_q.at(i - 1))
                    pool.tensor_tensor(seq(i - 1), seq(i - 1), gnb[:], ALU.add).then_inc(bias_in.sem, 1)
                if on(3):
                    pool.wait_ge(h_scale.sem, h_scale.at(i - 3))
                    pool.wait_ge(bias_in.sem, bias_in.at(i - 3))
                    pool.tensor_tensor(seq(i - 3), seq(i - 3), h_n[:], ALU.add).then_inc(h_out.sem, 1)
                if on(5):
                    pool.wait_ge(dest.sem, dest.at(i - 5))
                    pool.tensor_tensor(pay[:, v, DIM:C_ROW], r_me[:], r_i[:].to_broadcast([P, EXPERTS]), ALU.mult
                                       ).then_inc(weights.sem, 1)
                    pool.drain()
                    for k in range(TOP_K):
                        pool.indirect_dma_start(routed, bass.IndirectOffsetOnAxis(ap=r_dst[:, v, k:k + 1], axis=0),
                                                pay[:, v, :], None).then_inc(scatter[v].sem, 16)

            skewed(pool, SEQS, CROSS_LAGS, cross)

            for u in range(2):
                pool.wait_ge(store[u].sem, store[u].at(SEQS // 2 - 1))
            pool.wait_ge(trash_dma.sem, trash_dma.at(0))

            pool.wait_ge(tiling.sem, tiling.at(0))
            total = pool.value_load(t_first[0:1, EXPERTS:EXPERTS + 1], min_val=EXPERTS, max_val=MAX_TILES)

            def add(i):
                pool.wait_ge(y_out.sem, y_out.at(i))
                pool.wait_ge(rows_meta.sem, rows_meta.at(i))
                pool.tensor_copy(e_idx[:], e_id[:, bass.ds(parity(i), 1)].rearrange("p a k -> p (a k)")
                                 ).then_inc(idx_out.sem, 1)
                pool.drain()
                for k in range(BLOCKS):
                    pool.indirect_dma_start(out, bass.IndirectOffsetOnAxis(ap=e_idx[:, k:k + 1], axis=0),
                                            e_y[k][:], None, compute_op=ALU.add).then_inc(added.sem, 16)
                pool.wait_ge(added.sem, added.at(i))

            add(0)
            with pool.Fori(1, total) as i:
                add(i)

        @block.vector
        def _(dve):
            def attention(i, u, on, half_):
                if on(2):
                    dve.wait_ge(a_t.sem, a_t.at(i - 2))
                    if has(i - 3):
                        dve.wait_ge(a_v.sem, a_v.at(i - 3))
                    dve.tensor_copy(a_xnt[:].rearrange("p c b i -> p (c b i)"), ps_t[:, :]).then_inc(a_tc.sem, 1)
                if on(3):
                    dve.wait_ge(a_zz.sem, a_zz.at(i - 3))
                    if has(i - 4):
                        dve.wait_ge(a_e.sem, a_e.at(i - 4))
                    dve.scalar_tensor_tensor(a_z[:], ps_z[:, :].rearrange("p (k j) -> p k j", k=4), A_DH ** -0.5,
                                             block_mask.rearrange("p (a j) -> p a j", a=1).to_broadcast([P, 4, P]),
                                             ALU.mult, ALU.add).then_inc(a_zm.sem, 1)
                    dve.wait_ge(a_zm.sem, a_zm.at(i - 3, 1))
                    dve.tensor_reduce(a_max[:], a_z[:], AX.X, ALU.max).then_inc(a_zm.sem, 1)
                    dve.wait_ge(a_zm.sem, a_zm.at(i - 3, 2))
                    dve.tensor_scalar(a_neg[:], a_max[:], -1.0, None, ALU.mult).then_inc(a_zm.sem, 1)
                if on(4):
                    dve.wait_ge(a_o.sem, a_o.at(i - 4))
                    pair = res[:, bass.ds(2 * (i - 4), 2), :]
                    dve.tensor_tensor(pair, pair, ps_o[:, :].rearrange("p (b d) -> p b d", b=2),
                                      ALU.add).then_inc(a_res.sem, 1)
                if on(1):
                    dve.wait_ge(a_norm.sem, a_norm.at(i - 1))
                    if has(i - 2):
                        dve.wait_ge(a_t.sem, a_t.at(i - 2))
                    for b in range(2):
                        dve.tensor_scalar(a_xn[:, b], res[:, bass.ds(2 * (i - 1) + b, 1), :].rearrange(
                            "p a d -> p (a d)"), a_mv[:, b, 0:1], a_rstd[:, b:b + 1], ALU.subtract, ALU.mult
                            ).then_inc(a_ready.sem, 1)
                if on(0):
                    dve.wait_ge(ld_x[u].sem, ld_x[u].at(half_(0)))
                    if has(i - 1):
                        dve.wait_ge(a_norm.sem, a_norm.at(i - 1))
                    if has(i - 1):
                        dve.wait_ge(a_ready.sem, a_ready.at(i - 1))
                    for b in range(2):
                        dve.bn_stats(a_stat[:, b], res[:, 2 * i + b, :] if isinstance(i, int) else
                                     res[:, bass.ds(2 * i + b, 1), :].rearrange("p a d -> p (a d)")
                                     ).then_inc(a_stats.sem, 1)
                    dve.drain()
                    for b in range(2):
                        dve.bn_aggr(a_mv[:, b], a_stat[:, b]).then_inc(a_stats.sem, 1)
                if on(3):
                    dve.wait_ge(a_e.sem, a_e.at(i - 3))
                    if has(i - 4):
                        dve.wait_ge(a_pv.sem, a_pv.at(i - 4))
                    dve.reciprocal(a_inv[:], a_sum[:]).then_inc(a_sc.sem, 1)
                    dve.wait_ge(a_sc.sem, a_sc.at(i - 3, 1))
                    dve.tensor_tensor(a_pn[:], a_p[:], a_inv[:].rearrange("p (k a) -> p k a", a=1)
                                      .to_broadcast([P, 4, P]), ALU.mult).then_inc(a_sc.sem, 1)

            skewed(dve, PAIRS, 4, attention)

            def split_w(e, u, quarter):
                at = slice(quarter * WN // 4, (quarter + 1) * WN // 4)
                dve.wait_ge(w_hi_s.sem, w_hi_s.at(e, quarter + 1))
                dve.tensor_tensor(w_lo[u][:, at], w_in[:, u % 2, at], w_hi[u][:, at].bitcast(F32), ALU.subtract
                                  ).then_inc(w_lo_s.sem, 1)

            dve.wait_ge(ld_small.sem, ld_small.at(0))
            dve.memset(x_am[:], 0.0).then_inc(setup.sem, 1)
            dve.memset(x_hl[:].bitcast(F32), 0.0).then_inc(setup.sem, 1)
            dve.memset(v_c[:], 1.0 / TAU).then_inc(setup.sem, 1)
            dve.memset(c_x[:], 0.0).then_inc(setup.sem, 1)
            dve.memset(pay[:], 0.0)
            dve.memset(pad[:], 0.0)
            dve.memset(ones_bf[:], 1.0)
            dve.memset(t_ones[:], 1.0)
            dve.memset(t_scan[:], 0.0)
            dve.memset(n_half[:], -0.5)
            dve.memset(n_var[:], 1.0)
            dve.memset(n_mv[:], 1.0)
            dve.memset(gw_t[:], 0.0)
            dve.tensor_scalar(minus_bias[:], gate_bias[0:X_HEADS], -1.0, None, ALU.mult)
            dve.drain()
            dve.tensor_copy(pad[:, :, C_ROW].bitcast(I32), rows_id[:, SEQS:SEQS + BLOCKS]).then_inc(setup.sem, 1)
            dve.tensor_copy(sel_r[:], sel_in[:])
            dve.tensor_copy(ident_r[:], ident)
            dve.tensor_copy(causal_r[:], cst[:, C_CAUSAL:C_CAUSAL + P].rearrange("p (a j) -> p a j", a=1)
                            .to_broadcast([P, 4, P])).then_inc(setup.sem, 1)
            dve.tensor_copy(tri_before[:], cst[:, C_TRIX:C_TRIX + P])
            for column, at in ((0, X_HEADS), (32, 0)):
                heads_, out_ = slice(at, at + X_HEADS), slice(column, column + X_HEADS)
                dve.tensor_copy(gw_t[:, 0:CH, out_], gw[:, 0:CH, heads_])
                dve.tensor_tensor(gw_t[:, CH:, out_], gw[:, CH:2 * CH, heads_], gw[:, 2 * CH:3 * CH, heads_], ALU.add)
            dve.drain().then_inc(setup.sem, 1)
            dve.tensor_copy(r_base[:], cst[:, C_BASE:C_BASE + EXPERTS]).then_inc(setup.sem, 1)
            dve.drain()
            for e in range(2):
                for quarter in range(4):
                    split_w(e, e, quarter)

            def cross(i, u, on, half_):
                v = (u + 1) % 2
                norms = on(0) or on(4)
                if on(0):
                    dve.bn_stats(n_stat[:, 0], seq(i))
                if on(4):
                    dve.wait_ge(h_out.sem, h_out.at(i - 4))
                    dve.bn_stats(n_stat[:, 1], seq(i - 4))
                if on(3):
                    dve.wait_ge(expm.sem, expm.at(i - 3))
                    dve.tensor_tensor(h_max[:], h_abs[:], x_em[:], ALU.max)
                    dve.wait_ge(h_square.sem, h_square.at(i - 3))
                    dve.tensor_reduce(h_ss[:], h_sq[:], AX.X, ALU.add)
                dve.drain()
                if on(0):
                    dve.bn_aggr(n_mv[:, 0], n_stat[:, 0])
                if on(4):
                    dve.bn_aggr(n_mv[:, 1], n_stat[:, 1])
                if on(3):
                    dve.tensor_scalar(h_den[:], h_max[:], 1e-6, None, ALU.add)
                dve.drain()
                if norms:
                    if has(i - 1):
                        dve.wait_ge(rsqrt.sem, rsqrt.at(i - 1))
                    dve.tensor_scalar(n_var[:, 0:2], n_mv[:, :, 1], EPS, None, ALU.add)
                if on(3):
                    dve.scalar_tensor_tensor(h_e2[:], h_den[:], EPS, h_den[:], ALU.mult, ALU.mult)
                if on(5):
                    dve.wait_ge(logits.sem, logits.at(i - 5))
                    if has(i - 6):
                        dve.wait_ge(weights.sem, weights.at(i - 6))
                    dve.tensor_tensor(r_lg[:], ps_lg, rbias[:], ALU.add).then_inc(logits_b.sem, 1)
                dve.drain()
                if on(3):
                    dve.tensor_tensor(n_var[:, 2:], h_e2[:], h_ss[:], ALU.add)
                if norms:
                    dve.drain().then_inc(variances.sem, 1)
                if on(5):
                    dve.max(r_top[:], r_lg[:])
                    dve.drain()
                    dve.tensor_scalar(r_neg[:], r_top[:, 0:1], -1.0, None, ALU.mult)
                    dve.max_index(r_idx[:], r_top[:], r_lg[:]).then_inc(pick4.sem, 1)
                    dve.drain()
                if on(2):
                    if has(i - 3):
                        dve.wait_ge(heads.sem, heads.at(i - 3))
                    dve.wait_ge(scores.sem, scores.at(i - 2))
                    dve.wait_ge(decay.sem, decay.at(i - 2, 1))
                    dve.tensor_tensor(x_c[:, 0:4], ps_s[:, 0:4], x_d[:, 0:4], ALU.mult).then_inc(weigh.sem, 1)
                if on(5):
                    dve.tensor_tensor(r_hot[:], iota16.rearrange("p (a e) -> p a e", a=1).to_broadcast(
                        [P, TOP_K, EXPERTS]), r_idx[:, 0:TOP_K].rearrange("p (k a) -> p k a", a=1).to_broadcast(
                        [P, TOP_K, EXPERTS]), ALU.is_equal)
                    dve.drain()
                    with nc.allow_low_precision(reason="zeros and ones"):
                        dve.tensor_reduce(r_maskb[:], r_hot[:].rearrange("p k e -> p e k"), AX.X, ALU.add
                                          ).then_inc(masks.sem, 1)
                if on(1):
                    dve.wait_ge(gates_ln.sem, gates_ln.at(i - 1))
                    dve.tensor_tensor_scan(x_ncs[32:40, :], x_relu[:], x_ln[:], 0.0, ALU.add, ALU.add
                                           ).then_inc(ncs.sem, 1)
                if on(2):
                    dve.wait_ge(decay.sem, decay.at(i - 2))
                    dve.tensor_tensor(x_c[:, 4:8], ps_s[:, 4:8], x_d[:, 4:8], ALU.mult).then_inc(weigh.sem, 1)
                if on(1):
                    dve.wait_ge(ncs.sem, ncs.at(i - 1))
                    dve.scalar_tensor_tensor(x_am[0:X_HEADS, :], ps_i, gate_bias[32:40], x_ncs[32:40, :],
                                             ALU.add, ALU.add).then_inc(a_read.sem, 1)
                if norms:
                    dve.wait_ge(rsqrt.sem, rsqrt.at(i))
                    dve.scalar_tensor_tensor(n_mr[:], n_mv[:, :, 0], -1.0, n_rstd[:, 0:2], ALU.mult, ALU.mult
                                             ).then_inc(mean_r.sem, 1)
                if on(1):
                    dve.wait_ge(a_read.sem, a_read.at(i - 1))
                    dve.tensor_tensor_scan(x_am[32:40, :], x_am[0:X_HEADS, :], x_am[0:X_HEADS, :],
                                           -3e38, ALU.max, ALU.max).then_inc(a_run.sem, 1)
                if on(5):
                    dve.wait_ge(rexp.sem, rexp.at(i - 5))
                    dve.wait_ge(masks.sem, masks.at(i - 5))
                    dve.tensor_tensor(r_me[:], r_e[:], r_maskb[:], ALU.mult)
                    dve.tensor_copy(pay[:, v, C_ROW:C_ROW + 1].bitcast(I32), rows_id[:, bass.ds(i - 5, 1)])
                if on(3):
                    dve.wait_ge(h_factor.sem, h_factor.at(i - 3))
                    if has(i - 4):
                        dve.wait_ge(h_out.sem, h_out.at(i - 4))
                    dve.tensor_tensor(h_n[:].rearrange("p (h d) -> p h d", d=X_DH), ps_h[v][:, :, 0:X_DH],
                                      h_fw[:].rearrange("p (h d) -> p h d", d=X_DH), ALU.mult).then_inc(h_scale.sem, 1)
                if on(1):
                    dve.wait_ge(a_high.sem, a_high.at(i - 1))
                    dve.tensor_tensor(x_hl[64:104, v], x_am[:], x_hl[0:40, v].bitcast(F32), ALU.subtract
                                      ).then_inc(a_scan.sem, 1)
                    if has(i - 3):
                        dve.wait_ge(maxt.sem, maxt.at(i - 3))
                    dve.tensor_tensor(x_m[32:40, v], x_am[32:40, :], x_ncs[32:40, :], ALU.subtract
                                      ).then_inc(row_max.sem, 1)
                if on(5):
                    dve.drain()
                    dve.wait_ge(place.sem, place.at(i - 5))
                    dve.tensor_reduce(r_s[:], r_me[:], AX.X, ALU.add)
                    dve.tensor_tensor(r_pos[:], ps_pos, r_base[:], ALU.add)
                dve.drain()
                if on(5):
                    dve.reciprocal(r_i[:], r_s[:])
                    dve.tensor_tensor(r_base[:], r_base[:], ps_tot, ALU.add).then_inc(placed.sem, 1)
                    dve.tensor_tensor(r_dsel[:], r_hot[:], r_pos[:].rearrange("p (a e) -> p a e", a=1).to_broadcast(
                        [P, TOP_K, EXPERTS]), ALU.mult)
                if on(7):
                    dve.wait_ge(init_mm.sem, init_mm.at(i - 7))
                    if on(1):
                        dve.wait_ge(v_tc.sem, v_tc.at(i - 1))
                    if not (isinstance(i, int) and i < 9):
                        dve.wait_ge(store[v].sem, store[v].at(half_(7) - 1))
                    dve.tensor_tensor(o_init[:, v], ps_init, seq(i - 7), ALU.add).then_inc(init_add.sem, 1)
                dve.drain()
                if on(5):
                    with nc.allow_low_precision(reason="whole numbers"):
                        dve.tensor_reduce(r_dst[:, v], r_dsel[:], AX.X, ALU.add).then_inc(dest.sem, 1)
                dve.drain()

            skewed(dve, SEQS, CROSS_LAGS, cross)

            dve.tensor_tensor(t_cnt[:], r_base[:], cst[:, C_BASE:C_BASE + EXPERTS], ALU.subtract)
            dve.tensor_copy(t_end[:], r_base[:])
            dve.drain()
            dve.tensor_tensor(t_cmp[:], t_cnt[:].rearrange("p (e a) -> p e a", a=1).to_broadcast([P, EXPERTS, 16]),
                              cst[:, C_THR:C_THR + 256].rearrange("p (e k) -> p e k", k=16), ALU.is_gt)
            dve.drain()
            dve.tensor_reduce(t_num[:], t_cmp[:], AX.X, ALU.add)
            dve.drain()
            dve.tensor_scalar(t_num[:], t_num[:], 1.0, None, ALU.add)
            dve.drain()
            dve.tensor_tensor_scan(t_scan[:, 1:EXPERTS + 1], t_ones[:], t_num[:], 0.0, ALU.mult, ALU.add)
            dve.drain()
            dve.tensor_copy(t_first[:], t_scan[:]).then_inc(tiling.sem, 1)

            def meta(i):
                dve.wait_ge(ld_rows.sem, ld_rows.at(i))
                if has(i - 2):
                    dve.wait_ge(idx_out.sem, idx_out.at(i - 2))
                    dve.wait_ge(y_out.sem, y_out.at(i - 2))
                dve.tensor_copy(e_wt[:, bass.ds(parity(i), 1)].rearrange("p a k e -> p (a k) e"),
                                xt_rows[:, :, DIM:C_ROW])
                dve.tensor_copy(e_id[:, bass.ds(parity(i), 1)].rearrange("p a k -> p (a k)"),
                                xt_rows[:, :, C_ROW].bitcast(U32)).then_inc(rows_meta.sem, 1)

            def rows(i):
                dve.wait_ge(rows_hi.sem, rows_hi.at(i))
                dve.tensor_tensor(e_xl[:], ps_x, e_xh[:].bitcast(F32), ALU.subtract).then_inc(rows_lo.sem, 1)

            def tile(i, e, split=None):
                for m in range(HC):
                    if split and m < HC - 1:
                        split_w(*split, m)
                    if m == HC - 1:
                        meta(i + 1)
                    dve.wait_ge(gelu[m].sem, gelu[m].at(i))
                    if has(i - 1):
                        dve.wait_ge(down.sem, down.at(i - 1))
                    dve.tensor_tensor(e_hl[:, m], e_h[:, m], e_hh[:, m].bitcast(F32), ALU.subtract
                                      ).then_inc(h_lo[m].sem, 1)
                rows(i + 1)
                if split:
                    split_w(*split, 3)
                dve.wait_ge(down.sem, down.at(i))
                if has(i - 1):
                    dve.wait_ge(added.sem, added.at(i - 1))
                for k in range(BLOCKS):
                    dve.tensor_scalar(e_y[k][:], ps_y[k], e_wt[:, bass.ds(parity(i), 1), k, bass.ds(e, 1)].rearrange(
                        "p a b -> p (a b)"), None, ALU.mult).then_inc(y_out.sem, 1)

            def expert(e, u, splits=True):
                first, end = tiles_of(dve, e)
                tile(first, e, (e + 2, (u + 2) % 4) if splits else None)
                with dve.If(end > first + 1):
                    with dve.Fori(first + 1, end) as i:
                        tile(i, e)

            meta(0)
            rows(0)
            for e in range(4):
                expert(e, e)
            with dve.Fori(1, EXPERTS // 4 - 1) as four:
                for u in range(4):
                    expert(4 * four + u, u)
            for u in range(4):
                expert(EXPERTS - 4 + u, u, splits=u < 2)

        @block.scalar
        def _(act):
            act.preload_act_table_set("natural_log_exp_and_others")

            def attention(i, u, on, half_):
                if on(3):
                    act.wait_ge(a_zm.sem, a_zm.at(i - 3))
                    if has(i - 4):
                        act.wait_ge(a_sc.sem, a_sc.at(i - 4))
                    for k in range(4):
                        act.activation(a_p[:, k], a_z[:, k], ACT.Exp, bias=a_neg[:, k:k + 1],
                                       accum_out=a_sum[:, k:k + 1]).then_inc(a_e.sem, 1)
                if on(2):
                    if has(i - 3):
                        act.wait_ge(a_zz.sem, a_zz.at(i - 3))
                    for b in range(2):
                        act.wait_ge(a_proj.sem, a_proj.at(i - 2, b + 1))
                        act.copy(a_qk[:, b], ps_qk[b][:, :]).then_inc(a_projc.sem, 1)
                    act.wait_ge(a_v.sem, a_v.at(i - 2))
                    if has(i - 4):
                        act.wait_ge(a_pv.sem, a_pv.at(i - 4))
                    act.copy(a_vt[:, u].rearrange("p c b i -> p (c b i)"), ps_av).then_inc(a_vc.sem, 1)
                if on(3):
                    act.wait_ge(a_pv.sem, a_pv.at(i - 3))
                    if has(i - 4):
                        act.wait_ge(a_o.sem, a_o.at(i - 4))
                    act.copy(a_z2[:].rearrange("p c b i -> p (c b i)"), ps_z2[:, :]).then_inc(a_pvc.sem, 1)

            skewed(act, PAIRS, 4, attention)

            def split_w(e, u, half_of_e):
                act.wait_ge(ld_w[u % 2].sem, ld_w[u % 2].at(half_of_e))
                if has(e - 4):
                    act.wait_ge(w_done.sem, w_done.at(e - 4))
                for quarter in range(4):
                    at = slice(quarter * WN // 4, (quarter + 1) * WN // 4)
                    act.copy(w_hi[u][:, at], w_in[:, u % 2, at]).then_inc(w_hi_s.sem, 1)

            def refill(e, u):
                act.wait_ge(w_lo_s.sem, w_lo_s.at(e))
                load_w(act, e + 2, u % 2)

            for e in range(2):
                split_w(e, e, 0)
            for e in range(2):
                refill(e, e)
            act.wait_ge(setup.sem, setup.at(0))

            def cross(i, u, on, half_):
                v = (u + 1) % 2
                if on(3):
                    act.wait_ge(maxt.sem, maxt.at(i - 3))
                    if has(i - 4):
                        act.wait_ge(variances.sem, variances.at(i - 1))
                    act.activation(h_abs[:], ps_h[v][:, :, X_DH], ACT.Abs)
                    act.activation(x_em[:], ps_mt[v], ACT.Exp, scale=-1.0).then_inc(expm.sem, 1)
                    act.activation(h_sq[:], ps_h[v][:, :, 0:X_DH], ACT.Square, scale=X_DH ** -0.5
                                   ).then_inc(h_square.sem, 1)
                if on(1):
                    act.wait_ge(q_t.sem, q_t.at(i - 1))
                    if on(5):
                        act.wait_ge(rx_t.sem, rx_t.at(i - 5))
                    if has(i - 3):
                        act.wait_ge(scores.sem, scores.at(i - 3))
                        act.wait_ge(gates.sem, gates.at(i - 3))
                    act.copy(x_qt[:, v], ps_qt).then_inc(q_tc.sem, 1)
                if on(5):
                    act.wait_ge(rx_t.sem, rx_t.at(i - 5))
                    if has(i - 6):
                        act.wait_ge(logits.sem, logits.at(i - 6))
                    act.copy(r_xt[:], ps_xt).then_inc(rx_tc.sem, 1)
                if on(2):
                    for k in range(2):
                        act.wait_ge(args.sem, args.at(i - 2, k + 1))
                        if has(i - 3):
                            act.wait_ge(weigh.sem, weigh.at(i - 3, k + 1))
                        act.activation(x_d[:, 4 * k:4 * k + 4].rearrange("p h i -> p (h i)"), banks[2 + k], ACT.Exp
                                       ).then_inc(decay.sem, 1)
                if on(5):
                    act.wait_ge(pick4.sem, pick4.at(i - 5))
                    act.activation(r_e[:], r_lg[:], ACT.Exp, bias=r_neg[:]).then_inc(rexp.sem, 1)
                if on(1):
                    act.wait_ge(gates.sem, gates.at(i - 1))
                    if has(i - 2):
                        act.wait_ge(ncs.sem, ncs.at(i - 2))
                    act.activation(x_relu[:], ps_f, ACT.Relu, bias=minus_bias[:], scale=-1.0)
                    act.activation(x_abs[:], ps_f, ACT.Abs, bias=gate_bias[0:X_HEADS])
                    act.drain()
                    act.activation(x_ea[:], x_abs[:], ACT.Exp, scale=-1.0)
                    act.drain()
                    act.activation(x_ln[:], x_ea[:], ACT.Ln, bias=1.0).then_inc(gates_ln.sem, 1)
                    act.wait_ge(v_mm.sem, v_mm.at(i - 1))
                    if has(i - 3):
                        act.wait_ge(heads.sem, heads.at(i - 3))
                    act.mul(v_c[:, v, :, 0:X_DH], ps_v.rearrange("p (h d) -> p h d", d=X_DH), 1.0 / TAU
                            ).then_inc(v_tc.sem, 1)
                if on(6):
                    act.wait_ge(w_t.sem, w_t.at(i - 6))
                    if has(i - 7):
                        act.wait_ge(init_mm.sem, init_mm.at(i - 7))
                    act.copy(r_ct[:], ps_ct).then_inc(w_tc.sem, 1)
                if on(1):
                    act.wait_ge(a_run.sem, a_run.at(i - 1))
                    if has(i - 3):
                        act.wait_ge(args.sem, args.at(i - 3))
                    act.copy(x_hl[0:40, v], x_am[:]).then_inc(a_high.sem, 1)
                if on(0):
                    act.wait_ge(mean_r.sem, mean_r.at(i))
                    if has(i - 1):
                        act.wait_ge(q_t.sem, q_t.at(i - 1))
                    act.activation(x_q[:], seq(i), ACT.Identity, bias=n_mr[:, 0:1], scale=n_rstd[:, 0:1]
                                   ).then_inc(ln2_q.sem, 1)
                if on(4):
                    act.wait_ge(mean_r.sem, mean_r.at(i))
                    if not (isinstance(i, int) and i < 6):
                        act.wait_ge(scatter[u].sem, scatter[u].at(half_(4) - 1))
                    act.activation(pay[:, u, 0:DIM], seq(i - 4), ACT.Identity, bias=n_mr[:, 1:2], scale=n_rstd[:, 1:2]
                                   ).then_inc(ln3_x.sem, 1)

            skewed(act, SEQS, CROSS_LAGS, cross)

            def rows(i):
                act.wait_ge(rows_t.sem, rows_t.at(i))
                if has(i - 1):
                    act.wait_ge(up[HC - 1].sem, up[HC - 1].at(i - 1))
                act.copy(e_xh[:], ps_x).then_inc(rows_hi.sem, 1)

            def tile(i):
                for m in range(HC):
                    act.wait_ge(up[m].sem, up[m].at(i))
                    if has(i - 1):
                        act.wait_ge(h_lo[m].sem, h_lo[m].at(i - 1))
                        act.wait_ge(down.sem, down.at(i - 1))
                    act.activation(e_h[:, m], ps_hid[m], ACT.Gelu, bias=e_b1[:, m:m + 1])
                    act.activation(e_hh[:, m], ps_hid[m], ACT.Gelu, bias=e_b1[:, m:m + 1]
                                   ).then_inc(gelu[m].sem, 1)
                rows(i + 1)

            def expert(e, u, half_, splits=True, loads=True):
                if splits:
                    split_w(e + 2, (u + 2) % 4, half_ + 1)
                act.drain()
                act.copy(e_b1[:], b1_sb[:, bass.ds(e, 1)].rearrange("p a m -> p (a m)"))
                act.drain()
                first, end = tiles_of(act, e)
                tile(first)
                if loads:
                    refill(e + 2, u)
                with act.If(end > first + 1):
                    with act.Fori(first + 1, end) as i:
                        tile(i)

            act.wait_ge(ld_b1.sem, ld_b1.at(0))
            act.wait_ge(init_add.sem, init_add.at(SEQS - 1))
            act.wait_ge(tiling.sem, tiling.at(0))
            rows(0)
            for e in range(4):
                expert(e, e, e // 2)
            with act.Fori(1, EXPERTS // 4 - 1) as four:
                for u in range(4):
                    expert(4 * four + u, u, 2 * four + u // 2)
            for u in range(4):
                expert(EXPERTS - 4 + u, u, (EXPERTS - 4 + u) // 2, splits=u < 2, loads=False)

        @block.tensor
        def _(pe):
            pe.wait_ge(ld_cst.sem, ld_cst.at(0))
            pe.wait_ge(ld_wa.sem, ld_wa.at(0))

            def attention(i, u, on, half_):
                if on(2):
                    pe.wait_ge(a_ready.sem, a_ready.at(i - 2))
                    if has(i - 3):
                        pe.wait_ge(a_tc.sem, a_tc.at(i - 3))
                    for c in range(CH):
                        for b in range(2):
                            mm = pe.transpose(ps_t[:, (2 * c + b) * P:(2 * c + b + 1) * P],
                                              a_xn[:, b, c * P:(c + 1) * P], ident)
                    mm.then_inc(a_t.sem, 1)
                if on(3):
                    pe.wait_ge(a_projc.sem, a_projc.at(i - 3))
                    if has(i - 4):
                        pe.wait_ge(a_zm.sem, a_zm.at(i - 4))
                    for b in range(2):
                        for c in range(CH):
                            mm = pe.matmul(ps_z[:, (2 * b + c) * P:(2 * b + c + 1) * P],
                                           a_qk[:, b, DIM + c * P:DIM + (c + 1) * P],
                                           a_qk[:, b, c * P:(c + 1) * P], start=True, stop=True)
                    mm.then_inc(a_zz.sem, 1)
                if on(4):
                    pe.wait_ge(a_pvc.sem, a_pvc.at(i - 4))
                    if has(i - 5):
                        pe.wait_ge(a_res.sem, a_res.at(i - 5))
                    for b in range(2):
                        for c in range(CH):
                            mm = pe.matmul(ps_o[:, b * DIM:(b + 1) * DIM], a_z2[:, c, b], wo[:, c],
                                           start=(c == 0), stop=(c == CH - 1))
                    mm.then_inc(a_o.sem, 1)
                if on(2):
                    pe.wait_ge(a_tc.sem, a_tc.at(i - 2))
                    for b in range(2):
                        if has(i - 3):
                            pe.wait_ge(a_projc.sem, a_projc.at(i - 3, b + 1))
                        for c in range(CH):
                            mm = pe.matmul(ps_qk[b][:, :], a_xnt[:, c, b], wqk[:, c], start=(c == 0), stop=(c == 1))
                        mm.then_inc(a_proj.sem, 1)
                    if has(i - 3):
                        pe.wait_ge(a_vc.sem, a_vc.at(i - 3))
                    for m in range(CH):
                        for c in range(CH):
                            mm = pe.matmul(ps_av[:, m * 2 * P:(m + 1) * 2 * P], wv[:, c, m * P:(m + 1) * P],
                                           a_xnt[:, c].rearrange("p b i -> p (b i)"), start=(c == 0), stop=(c == 1))
                    mm.then_inc(a_v.sem, 1)
                if on(3):
                    pe.wait_ge(a_sc.sem, a_sc.at(i - 3))
                    pe.wait_ge(a_vc.sem, a_vc.at(i - 3))
                    if has(i - 4):
                        pe.wait_ge(a_pvc.sem, a_pvc.at(i - 4))
                    for c in range(CH):
                        for b in range(2):
                            mm = pe.matmul(ps_z2[:, (2 * c + b) * P:(2 * c + b + 1) * P], a_pn[:, 2 * b + c],
                                           a_vt[:, (u + 1) % 2, c, b], start=True, stop=True)
                    mm.then_inc(a_pv.sem, 1)

            skewed(pe, PAIRS, 4, attention)
            pe.wait_ge(setup.sem, setup.at(0))
            if has(PAIRS - 1):
                pe.wait_ge(a_res.sem, a_res.at(PAIRS - 1))
            if has(PAIRS - 1):
                pe.wait_ge(a_pvc.sem, a_pvc.at(PAIRS - 1))

            def cross(i, u, on, half_):
                v = (u + 1) % 2
                if on(1):
                    pe.wait_ge(ln2_q.sem, ln2_q.at(i - 1))
                    if has(i - 2):
                        pe.wait_ge(v_tc.sem, v_tc.at(i - 2))
                    if on(8):
                        pe.wait_ge(init_add.sem, init_add.at(i - 8))
                    for c in range(CH):
                        mm = pe.transpose(ps_qt[:, c], x_q[:, c * P:(c + 1) * P], ident)
                    mm.then_inc(q_t.sem, 1)
                if on(5):
                    pe.wait_ge(ln3_x.sem, ln3_x.at(i - 5))
                    if on(8):
                        pe.wait_ge(init_add.sem, init_add.at(i - 8))
                    for c in range(CH):
                        mm = pe.transpose(ps_xt[:, c], pay[:, v, c * P:(c + 1) * P], ident)
                    mm.then_inc(rx_t.sem, 1)

                def decay_args(k):
                    pe.wait_ge(a_scan.sem, a_scan.at(i - 2))
                    if has(i - 3):
                        pe.wait_ge(decay.sem, decay.at(i - 3, k + 1))
                    pe.matmul(ps_arg[k], ident_r[:], causal_r[:].rearrange("p h i -> p (h i)"),
                              start=True, stop=False)
                    pe.matmul(ps_arg[k], x_hl[:, u], sel_a[:, k * 4 * P:(k + 1) * 4 * P], start=False, stop=False)
                    for h in range(4):
                        mm = pe.matmul(ps_arg[k][:, h * P:(h + 1) * P], sel_max[:, 4 * k + h], x_hl[:, u],
                                       start=False, stop=(h == 3))
                    mm.then_inc(args.sem, 1)

                if on(2):
                    decay_args(0)
                if on(5):
                    pe.wait_ge(rx_tc.sem, rx_tc.at(i - 5))
                    if on(6):
                        pe.wait_ge(placed.sem, placed.at(i - 6))
                    for c in range(CH):
                        mm = pe.matmul(ps_lg, r_xt[:, c], rw[:, c], start=(c == 0), stop=(c == 1))
                    mm.then_inc(logits.sem, 1)
                if on(2):
                    decay_args(1)
                if on(1):
                    pe.wait_ge(q_tc.sem, q_tc.at(i - 1))
                    pe.wait_ge(ld_ct[v].sem, ld_ct[v].at(half_(1)))
                    if has(i - 2):
                        pe.wait_ge(a_read.sem, a_read.at(i - 2))
                    if on(5):
                        pe.wait_ge(logits_b.sem, logits_b.at(i - 5))
                    for n, a in enumerate([x_qt[:, v, c] for c in range(CH)] + [c_t[:, v, c] for c in range(CH)]):
                        mm = pe.matmul(ps_gates, gw_t[:, n], a, start=(n == 0), stop=(n == 3))
                    mm.then_inc(gates.sem, 1)
                if on(7):
                    pe.wait_ge(w_tc.sem, w_tc.at(i - 7))
                    if on(8):
                        pe.wait_ge(init_add.sem, init_add.at(i - 8))
                    if on(5):
                        pe.wait_ge(rx_tc.sem, rx_tc.at(i - 5))
                    pe.matmul(ps_init, r_ct[:], b2_sb[:], start=True, stop=True).then_inc(init_mm.sem, 1)
                if on(1):
                    if on(5):
                        pe.wait_ge(rx_tc.sem, rx_tc.at(i - 5))
                    for c in range(CH):
                        mm = pe.matmul(ps_v[:, c * P:(c + 1) * P], c_t[:, v, c], centre, start=True, stop=True)
                    mm.then_inc(v_mm.sem, 1)

                def head_rows(k):
                    pe.wait_ge(weigh.sem, weigh.at(i - 2, k + 1))
                    for h in range(4 * k, 4 * k + 4):
                        mm = pe.matmul(ps_h[u][:, h], x_c[:, h], v_c[:, u, h], start=True, stop=True)
                    return mm

                if on(2):
                    pe.wait_ge(row_max.sem, row_max.at(i - 2))
                    pe.wait_ge(v_tc.sem, v_tc.at(i - 2))
                    if has(i - 4):
                        pe.wait_ge(h_scale.sem, h_scale.at(i - 4))
                    head_rows(0)
                if on(6):
                    pe.wait_ge(weights.sem, weights.at(i - 6))
                    if on(5):
                        pe.wait_ge(logits_b.sem, logits_b.at(i - 5))
                    if on(1):
                        pe.wait_ge(gates_ln.sem, gates_ln.at(i - 1))
                    pe.transpose(ps_ct, pay[:, u, DIM:C_ROW], ident).then_inc(w_t.sem, 1)
                if on(2):
                    head_rows(1).then_inc(heads.sem, 1)
                    pe.transpose(ps_mt[u], x_m[32:40, u], cst[32:40, C_ID + 32:C_ID + 40]).then_inc(maxt.sem, 1)
                if on(5):
                    pe.wait_ge(masks.sem, masks.at(i - 5))
                    if on(1):
                        pe.wait_ge(a_read.sem, a_read.at(i - 1))
                    else:
                        pe.wait_ge(logits_b.sem, logits_b.at(i - 5))
                    if on(6):
                        pe.wait_ge(w_tc.sem, w_tc.at(i - 6))
                    pe.matmul(ps_pos, tri_before[:], r_maskb[:], start=True, stop=True)
                    pe.matmul(ps_tot, ones_bf[:], r_maskb[:], start=True, stop=True).then_inc(place.sem, 1)
                if on(1):
                    if has(i - 2):
                        pe.wait_ge(weigh.sem, weigh.at(i - 2))
                    pe.wait_ge(ld_cx[v].sem, ld_cx[v].at(half_(1)))
                    for h in range(X_HEADS):
                        mm = pe.matmul(ps_s[:, h], c_x[:, v, h // 4, h % 4], x_qt[:, v, h // 4], start=True, stop=True)
                    mm.then_inc(scores.sem, 1)

            skewed(pe, SEQS, CROSS_LAGS, cross)

            def turn(i):
                pe.wait_ge(ld_rows.sem, ld_rows.at(i))
                if has(i - 1):
                    pe.wait_ge(rows_lo.sem, rows_lo.at(i - 1))
                for c in range(CH):
                    for k in range(BLOCKS):
                        mm = pe.transpose(ps_x[:, c, k * P:(k + 1) * P], xt_rows[:, k, c * P:(c + 1) * P], ident)
                mm.then_inc(rows_t.sem, 1)

            def products(out_, pairs, first, last):
                todo = [p for (ah, al), (bh, bl) in pairs for p in ((ah, bh), (ah, bl), (al, bh))]
                for n, (a, b) in enumerate(todo):
                    mm = pe.matmul(out_, a, b, start=(first and n == 0), stop=(last and n == len(todo) - 1))
                return mm

            def tile(i, e, u):
                def w_up(c, m):
                    at = slice(c * HID + m * P, c * HID + (m + 1) * P)
                    return w_hi[u][:, at], w_lo[u][:, at]

                def w_down(m):
                    at = slice(W1N + m * DIM, W1N + (m + 1) * DIM)
                    return w_hi[u][:, at], w_lo[u][:, at]

                def up_(m):
                    if has(i - 1):
                        pe.wait_ge(gelu[m].sem, gelu[m].at(i - 1))
                    products(ps_hid[m], [(w_up(c, m), (e_xh[:, c], e_xl[:, c])) for c in range(CH)],
                             True, True).then_inc(up[m].sem, 1)

                def down_(m):
                    pe.wait_ge(h_lo[m].sem, h_lo[m].at(i))
                    for k in range(BLOCKS):
                        at = slice(k * P, (k + 1) * P)
                        mm = products(ps_y[k], [((e_hh[:, m, at], e_hl[:, m, at]), w_down(m))],
                                      m == 0, m == HC - 1)
                    return mm

                pe.wait_ge(w_lo_s.sem, w_lo_s.at(e))
                pe.wait_ge(rows_lo.sem, rows_lo.at(i))
                for m in range(HC):
                    up_(m)
                turn(i + 1)
                if has(i - 1):
                    pe.wait_ge(y_out.sem, y_out.at(i - 1))
                for m in range(HC - 1):
                    down_(m)
                down_(HC - 1).then_inc(down.sem, 1)

            def expert(e, u):
                first, end = tiles_of(pe, e)
                tile(first, e, u)
                with pe.If(end > first + 1):
                    with pe.Fori(first + 1, end) as i:
                        tile(i, e, u)
                pe.drain().then_inc(w_done.sem, 1)

            pe.wait_ge(tiling.sem, tiling.at(0))
            turn(0)
            for e in range(4):
                expert(e, e)
            with pe.Fori(1, EXPERTS // 4) as four:
                for u in range(4):
                    expert(4 * four + u, u)


def kernel(x, ctx_1024, L0_attn_Wq, L0_attn_Wk, L0_attn_Wv, L0_attn_Wo, L0_xattn_Wi_w, L0_xattn_Wi_b,
           L0_xattn_Wf_w, L0_xattn_Wf_b, L0_xattn_gn_w, L0_xattn_gn_b, L0_ffn_router_w, L0_ffn_router_b,
           L0_ffn_w1, L0_ffn_b1, L0_ffn_w2, L0_ffn_b2):
    import concourse.bacc as bacc
    from concourse.bass_utils import run_bass_kernel_spmd

    consts, selectors, row_ids = shape_constants()
    arrays = {
        "x": x, "ctx_t": np.transpose(ctx_1024, (0, 2, 1)),
        "w_qk_t": np.concatenate([np.transpose(L0_attn_Wq), np.transpose(L0_attn_Wk)], axis=1),
        "w_v_t": np.transpose(L0_attn_Wv), "w_o_t": np.transpose(L0_attn_Wo),
        "gate_w_t": np.transpose(np.concatenate([L0_xattn_Wi_w, L0_xattn_Wf_w], axis=0)),
        "gate_b": np.concatenate([L0_xattn_Wi_b, L0_xattn_Wf_b]),
        "gn_w": L0_xattn_gn_w, "gn_b": L0_xattn_gn_b,
        "router_w": L0_ffn_router_w, "router_b": L0_ffn_router_b,
        "w1": L0_ffn_w1, "b1": np.transpose(np.reshape(L0_ffn_b1, (EXPERTS, HC, P)), (2, 0, 1)),
        "w2": L0_ffn_w2, "b2": L0_ffn_b2,
        "consts": consts, "selectors": selectors, "row_ids": row_ids,
    }
    nc = bacc.Bacc("TRN2", target_bir_lowering=False, num_devices=1)
    ins, args = {}, []
    for name, a in arrays.items():
        ins[name] = np.ascontiguousarray(a)
        args.append(nc.dram_tensor(name, ins[name].shape, mybir.dt.from_np(ins[name].dtype),
                                   kind="ExternalInput").ap())
    args.append(nc.dram_tensor("out_rows", (OUT_ROWS, DIM), F32, kind="ExternalOutput").ap())
    decoder_layer(nc, *args)
    r = run_bass_kernel_spmd(nc, [ins], core_ids=[0])
    return r.results[0]["out_rows"][0:TOKENS].reshape(SEQS, LEN, DIM)
```

```python
import concourse.bass as bass
import concourse.mybir as mybir
import numpy as np
from contextlib import ExitStack

F32 = mybir.dt.float32
F32R = mybir.dt.float32r
BF16 = mybir.dt.bfloat16
U32 = mybir.dt.uint32
I32 = mybir.dt.int32
ALU = mybir.AluOpType
ACT = mybir.ActivationFunctionType
AX = mybir.AxisListType

P = 128
SEQS, LEN, DIM = 32, 128, 256
CH = DIM // P
A_HEADS, X_HEADS = 16, 8
A_DH, X_DH = DIM // A_HEADS, DIM // X_HEADS
TOKENS = SEQS * LEN
EXPERTS, TOP_K, HID = 16, 4, 512
HC = HID // P
W1N = CH * HID
WN = W1N + HC * DIM
EPS = 1e-5
TAU = X_DH ** 0.5
MASKED = -1e30

ROWS = 256
BLOCKS = ROWS // P
REGION = TOKENS + ROWS
C_ROW = DIM + EXPERTS
PAY = C_ROW + 16
MAX_TILES = TOKENS * TOP_K // ROWS + EXPERTS
OUT_ROWS = TOKENS + ROWS
CROSS_LAGS = 8
NORMS = 2 + X_HEADS
GROUPS = X_DH + 1

C_ID, C_CAUSAL, C_BLOCK, C_TRIX, C_CENTRE = (P * k for k in range(5))
C_IOTA = 5 * P
C_BASE = C_IOTA + EXPERTS
C_THR = C_BASE + EXPERTS
C_SEL = C_THR + EXPERTS * TOKENS // ROWS
C_END = C_SEL + 2 * X_HEADS
HL_ROWS = 104


def shape_constants():
    c = np.zeros((P, C_END), np.float32)
    p, q = np.arange(P)[:, None], np.arange(P)[None, :]
    c[:, C_ID:C_ID + P] = p == q
    c[:, C_CAUSAL:C_CAUSAL + P] = np.where(p <= q, 0.0, MASKED)
    c[:, C_BLOCK:C_BLOCK + P] = np.where(p // A_DH == q // A_DH, 0.0, MASKED)
    c[:, C_TRIX:C_TRIX + P] = p < q
    c[:, C_CENTRE:C_CENTRE + P] = (p == q) - np.where(p // X_DH == q // X_DH, 1.0 / X_DH, 0.0)
    c[:, C_IOTA:C_IOTA + EXPERTS] = np.arange(EXPERTS)
    c[:, C_BASE:C_BASE + EXPERTS] = np.arange(EXPERTS) * REGION
    c[:, C_THR:C_SEL] = np.tile(ROWS * np.r_[np.arange(1, 16), 10 ** 9], EXPERTS)
    for h in range(X_HEADS):
        c[[32 + h, 96 + h], C_SEL + h] = -1.0
        c[[h, 64 + h], C_SEL + X_HEADS + h] = 1.0
    rows = np.arange(SEQS + BLOCKS, dtype=np.int32)[None, :] * P + np.arange(P, dtype=np.int32)[:, None]
    return c, rows


class Step:

    def __init__(self, sem, n=1):
        self.sem, self.n = sem, n

    def at(self, t, j=None):
        return self.n * t + (self.n if j is None else j)


def has(t):
    return not (isinstance(t, int) and t < 0)


def skewed(engine, items, lags, body):
    def peeled(i):
        body(i, i % 2, lambda lag: 0 <= i - lag < items, lambda lag: (i - lag) // 2)

    first, last = lags + 2 - lags % 2, items - items % 2
    for i in range(first):
        peeled(i)
    with engine.Fori(first // 2, last // 2) as k:
        for u in range(2):
            body(2 * k + u, u, lambda lag: True, lambda lag: k + (u - lag) // 2)
    for i in range(last, items + lags):
        peeled(i)


def decoder_layer(nc, x, ctx_t, w_qk_t, w_v_t, w_o_t, gate_w_t, gate_b, gn_w, gn_b,
                  router_w, router_b, w1, b1, w2, b2, consts, row_ids, out):
    stack = ExitStack()
    with stack:
        def sb(name, shape, dt=F32):
            return stack.enter_context(nc.sbuf_tensor(name, shape, dt))

        def step(name, n=1):
            return Step(stack.enter_context(nc.semaphore(name)), n)

        psum = stack.enter_context(nc.psum_tensor("psum", [P, 8, 512], F32))
        banks = [psum[:, i, :] for i in range(8)]

        routed = nc.dram_tensor("routed_rows", [EXPERTS * REGION, PAY], F32, kind="Internal").ap()

        cst = sb("cst", [P, C_END])
        ident = cst[:, C_ID:C_ID + P]
        block_mask = cst[:, C_BLOCK:C_BLOCK + P]
        centre = cst[:, C_CENTRE:C_CENTRE + P]
        iota16 = cst[:, C_IOTA:C_IOTA + EXPERTS]
        sel_r = sb("sel_r", [HL_ROWS, 2 * X_HEADS * P], F32R)
        sel_max = sel_r[:, 0:X_HEADS * P].rearrange("k (h j) -> k h j", h=X_HEADS)
        sel_a = sel_r[:, X_HEADS * P:2 * X_HEADS * P]
        ident_r = sb("ident_r", [P, P], F32R)
        causal_r = sb("causal_r", [P, 4, P], F32R)
        tri_before = sb("tri_before", [P, P], BF16)
        ones_bf = sb("ones_bf", [P, P], BF16)
        half = sb("half", [P, X_HEADS])
        eps = sb("eps", [P, X_HEADS])
        gate_bias = sb("gate_bias", [40, 1])
        minus_bias = sb("minus_bias", [X_HEADS, 1])
        gnw = sb("gnw", [P, DIM])
        gnb = sb("gnb", [P, DIM])
        rbias = sb("rbias", [P, EXPERTS])
        rw = sb("rw", [P, CH, EXPERTS])
        b2_sb = sb("b2_sb", [EXPERTS, DIM])
        b1_sb = sb("b1_sb", [P, EXPERTS, HC])
        gw = sb("gw", [P, 3 * CH, 2 * X_HEADS])
        gw_t = sb("gw_t", [P, 2 * CH, 40])

        ps_t, ps_qk, ps_av, ps_z, ps_z2, ps_o = banks[0], banks[1:3], banks[3], banks[4], banks[5], banks[6]

        ld_cst = step("ld_cst", 16)
        ld_x = [step(f"ld_x{u}", 16) for u in range(2)]
        ld_wa = step("ld_wa", 48)
        ld_small = step("ld_small", 16 * 9)
        ld_b1 = step("ld_b1", 16)
        cst_ready = step("cst_ready", 2)

        a_stats = step("a_stats", 4)
        a_norm = step("a_norm", 2)
        a_ready = step("a_ready", 2)
        a_t = step("a_t")
        wa_hi = step("wa_hi", 3)
        wa_lo = step("wa_lo", 3)
        a_th = step("a_th")
        a_pvh = step("a_pvh")
        a_tc = step("a_tc")
        a_proj = step("a_proj", 2)
        a_projc = step("a_projc", 2)
        a_v = step("a_v")
        a_vc = step("a_vc")
        a_zz = step("a_zz")
        a_zm = step("a_zm", 3)
        a_e = step("a_e", 4)
        a_sc = step("a_sc", 2)
        a_pv = step("a_pv")
        a_pvc = step("a_pvc")
        a_o = step("a_o")
        a_res = step("a_res")
        PAIRS = SEQS // 2

        n_stat = sb("n_stat", [P, 2, 6])
        n_mv = sb("n_mv", [P, 2, 2])
        n_var = sb("n_var", [P, NORMS])
        n_rstd = sb("n_rstd", [P, NORMS])
        n_half = sb("n_half", [P, NORMS])
        n_mr = sb("n_mr", [P, 2])
        x_q = sb("x_q", [P, DIM])
        h_abs = sb("h_abs", [P, X_HEADS])
        h_e2 = sb("h_e2", [P, X_HEADS])
        h_fw = sb("h_fw", [P, DIM])
        c_t = sb("c_t", [P, 2, CH, P])
        c_x = sb("c_x", [P, 2, CH, 4, P])
        v_c = sb("v_c", [P, 2, X_HEADS, GROUPS])
        x_qt = sb("x_qt", [P, 2, CH, P])
        x_abs = sb("x_abs", [X_HEADS, P])
        x_relu = sb("x_relu", [X_HEADS, P])
        x_ncs = sb("x_ncs", [40, P])
        x_m = sb("x_m", [40, 2, P])
        x_ea = sb("x_ea", [X_HEADS, P])
        x_ln = sb("x_ln", [X_HEADS, P])
        x_am = sb("x_am", [40, P])
        x_hl = sb("x_hl", [HL_ROWS, 2, P], F32R)
        x_d = sb("x_d", [P, X_HEADS, P])
        x_c = sb("x_c", [P, X_HEADS, P])
        x_em = sb("x_em", [P, X_HEADS])
        h_sq = sb("h_sq", [P, X_HEADS, X_DH])
        h_max = sb("h_max", [P, X_HEADS])
        h_den = sb("h_den", [P, X_HEADS])
        h_ss = sb("h_ss", [P, X_HEADS])
        h_n = sb("h_n", [P, DIM])
        pay = sb("pay", [P, 2, PAY])
        r_xt = sb("r_xt", [P, CH, P])
        r_lg = sb("r_lg", [P, EXPERTS])
        r_top = sb("r_top", [P, 8])
        r_idx = sb("r_idx", [P, 8], U32)
        r_neg = sb("r_neg", [P, 1])
        r_e = sb("r_e", [P, EXPERTS])
        r_hot = sb("r_hot", [P, TOP_K, EXPERTS])
        r_maskb = sb("r_maskb", [P, EXPERTS], BF16)
        r_me = sb("r_me", [P, EXPERTS])
        r_s = sb("r_s", [P, 1])
        r_i = sb("r_i", [P, 1])
        r_base = sb("r_base", [P, EXPERTS])
        r_pos = sb("r_pos", [P, EXPERTS])
        r_dsel = sb("r_dsel", [P, TOP_K, EXPERTS])
        r_dst = sb("r_dst", [P, 2, TOP_K], U32)
        r_ct = sb("r_ct", [EXPERTS, P])
        o_init = sb("o_init", [P, 2, DIM])
        rows_id = sb("rows_id", [P, SEQS + BLOCKS], I32)
        pad = sb("pad", [P, BLOCKS, PAY])
        t_ones = sb("t_ones", [P, EXPERTS])
        t_cnt = sb("t_cnt", [P, EXPERTS])
        t_cmp = sb("t_cmp", [P, EXPERTS, 16])
        t_num = sb("t_num", [P, EXPERTS])
        t_scan = sb("t_scan", [P, EXPERTS + 1])
        t_first = sb("t_first", [P, EXPERTS + 1], I32)
        t_end = sb("t_end", [P, EXPERTS], I32)

        ps_s = psum[:, 0:2, :].rearrange("p k (h i) -> p (k h) i", h=4)
        ps_arg = banks[2:4]
        ps_qt = banks[4][:, 0:256].rearrange("p (c i) -> p c i", c=CH)
        ps_xt = banks[4][:, 256:512].rearrange("p (c i) -> p c i", c=CH)
        ps_v = banks[4][:, 0:256]
        ps_init = banks[4][:, 256:512]
        ps_h = [banks[5 + u][:, 0:X_HEADS * GROUPS].rearrange("p (h d) -> p h d", h=X_HEADS) for u in range(2)]
        ps_mt = [banks[5 + u][:, 288:296] for u in range(2)]
        ps_lg, ps_pos, ps_tot = (banks[7][:, 16 * k:16 * k + 16] for k in range(3))
        ps_f = banks[7][0:X_HEADS, 128:256]
        ps_i = banks[7][32:32 + X_HEADS, 128:256]
        ps_gates = banks[7][0:40, 128:256]
        ps_ct = banks[7][0:EXPERTS, 256:384]

        ld_ct = [step(f"ld_ct{u}", 16) for u in range(2)]
        ld_cx = [step(f"ld_cx{u}", 64) for u in range(2)]
        setup = step("setup", 8)
        variances = step("variances")
        rsqrt = step("rsqrt")
        mean_r = step("mean_r")
        ln2_q = step("ln2_q")
        q_t = step("q_t")
        q_tc = step("q_tc")
        v_mm = step("v_mm")
        v_tc = step("v_tc")
        gates = step("gates")
        gates_ln = step("gates_ln")
        a_read = step("a_read")
        a_run = step("a_run")
        row_max = step("row_max")
        ncs = step("ncs")
        a_high = step("a_high")
        a_scan = step("a_scan")
        scores = step("scores", 2)
        maxt = step("maxt")
        expm = step("expm")
        h_square = step("h_square")
        heads = step("heads")
        h_factor = step("h_factor")
        h_scale = step("h_scale")
        bias_in = step("bias_in")
        h_out = step("h_out")
        ln3_x = step("ln3_x")
        rx_t = step("rx_t")
        rx_tc = step("rx_tc")
        logits = step("logits")
        logits_b = step("logits_b")
        pick4 = step("pick4")
        rexp = step("rexp")
        weights = step("weights")
        masks = step("masks")
        place = step("place")
        placed = step("placed")
        dest = step("dest")
        w_t = step("w_t")
        w_tc = step("w_tc")
        init_mm = step("init_mm")
        init_add = step("init_add")
        args = step("args", 2)
        decay = step("decay", 2)
        weigh = step("weigh", 2)
        scatter = [step(f"scatter{u}", 16 * TOP_K) for u in range(2)]
        store = [step(f"store{u}", 16) for u in range(2)]
        trash_dma = step("trash_dma", 16)
        tiling = step("tiling")
        tail = step("tail", 16)

        w_in = sb("w_in", [P, 2, WN])
        attention_memory = ExitStack()

        def sb_a(name, shape, dt=F32):
            return attention_memory.enter_context(nc.sbuf_tensor(name, shape, dt))

        wqk = sb_a("wqk", [P, CH, 2 * DIM])
        wv = sb_a("wv", [P, CH, DIM])
        wo = sb_a("wo", [P, CH, DIM])
        a_stat = sb_a("a_stat", [P, 2, 6])
        a_mv = sb_a("a_mv", [P, 2, 2])
        a_var = sb_a("a_var", [P, 2])
        a_rstd = sb_a("a_rstd", [P, 2])
        a_xn = sb_a("a_xn", [P, 2, DIM])
        wqk_hi, wqk_lo = (sb_a(f"wqk_{part}", [P, CH, 2 * DIM], F32R) for part in ("hi", "lo"))
        wv_hi, wv_lo = (sb_a(f"wv_{part}", [P, CH, DIM], F32R) for part in ("hi", "lo"))
        wo_hi, wo_lo = (sb_a(f"wo_{part}", [P, CH, DIM], F32R) for part in ("hi", "lo"))
        a_xh, a_xl = (sb_a(f"a_x{part}", [P, CH, 2, P], F32R) for part in ("hi", "lo"))
        a_qk = sb_a("a_qk", [P, 2, 2 * DIM])
        a_vt = sb_a("a_vt", [P, 2, CH, 2, P])
        a_z = sb_a("a_z", [P, 4, P])
        a_p = sb_a("a_p", [P, 4, P])
        a_pn = sb_a("a_pn", [P, 4, P])
        a_max = sb_a("a_max", [P, 4])
        a_neg = sb_a("a_neg", [P, 4])
        a_sum = sb_a("a_sum", [P, 4])
        a_inv = sb_a("a_inv", [P, 4])
        a_zh, a_zl = (sb_a(f"a_z2{part}", [P, CH, 2, P], F32R) for part in ("hi", "lo"))
        attention_memory.close()

        parts = [sb(f"w_parts{k}", [P, WN], F32R)[:] for k in range(4)]
        xt_rows = sb("xt_rows", [P, BLOCKS, PAY])
        e_wt = sb("e_wt", [P, 2, BLOCKS, EXPERTS])
        e_id = sb("e_id", [P, 2, BLOCKS], U32)
        e_xh = sb("e_xh", [P, CH, ROWS], F32R)
        e_xl = sb("e_xl", [P, CH, ROWS], F32R)
        e_b1 = sb("e_b1", [P, HC])
        e_h = sb("e_h", [P, HC, ROWS])
        e_hh = sb("e_hh", [P, HC, ROWS], F32R)
        e_hl = sb("e_hl", [P, HC, ROWS], F32R)
        e_y = [sb(f"e_y{k}", [P, DIM]) for k in range(BLOCKS)]
        e_idx = sb("e_idx", [P, BLOCKS], U32)
        with nc.sbuf_tensor("res", [P, SEQS, DIM], F32) as res:
            pass
        parts += [sb(f"w_parts{k}", [P, WN], F32R)[:] for k in range(4, 8)]
        w_hi, w_lo = parts[0::2], parts[1::2]
        ps_hid = [banks[m][:, 0:ROWS] for m in range(HC)]
        ps_y = [banks[HC + k][:, 0:DIM] for k in range(BLOCKS)]
        ps_x = banks[HC + BLOCKS].rearrange("p (c r) -> p c r", c=CH)

        ld_w = [step(f"ld_w{u}", 32) for u in range(2)]
        w_hi_s = step("w_hi_s", 4)
        w_lo_s = step("w_lo_s", 4)
        ld_rows = step("ld_rows", 16)
        rows_t = step("rows_t")
        rows_hi = step("rows_hi")
        rows_lo = step("rows_lo")
        rows_meta = step("rows_meta")
        up = [step(f"up{m}") for m in range(HC)]
        gelu = [step(f"gelu{m}") for m in range(HC)]
        h_lo = [step(f"h_lo{m}") for m in range(HC)]
        down = step("down")
        y_out = step("y_out", BLOCKS)
        idx_out = step("idx_out")
        added = step("added", 16 * BLOCKS)

        x_v = x.rearrange("b t d -> t b d")
        out_v = out[0:TOKENS, :].rearrange("(b t) d -> t b d", t=P)
        block = stack.enter_context(nc.Block())

        def tile_bounds(engine, four):
            def bound(k):
                return engine.value_load(t_first[0:1, bass.ds(4 * four + k, 1)],
                                         min_val=4 * (four if isinstance(four, int) else 1) + k, max_val=MAX_TILES)

            first = 0 if isinstance(four, int) and four == 0 else bound(0)
            return [first] + [bound(k) for k in range(1, 5)]

        def load_w(engine, e, u):
            engine.dma_start(w_in[:, u, 0:W1N].rearrange("p (c n) -> p c n", c=CH),
                             w1[bass.ds(e, 1)].rearrange("a (c p) n -> p (a c) n", p=P)).then_inc(ld_w[u].sem, 16)
            engine.dma_start(w_in[:, u, W1N:].rearrange("p (c n) -> p c n", c=HC),
                             w2[bass.ds(e, 1)].rearrange("a (c p) n -> p (a c) n", p=P)).then_inc(ld_w[u].sem, 16)

        def seq(t):
            return res[:, bass.ds(t, 1), :].rearrange("p a d -> p (a d)")

        @block.sync
        def _(sp):
            sp.dma_start(cst[:], consts).then_inc(ld_cst.sem, 16)

            def load_x(p, u):
                sp.dma_start(res[:, bass.ds(2 * p, 2), :], x_v[:, bass.ds(2 * p, 2), :]).then_inc(ld_x[u].sem, 16)

            load_x(0, 0)
            load_x(1, 1)
            sp.dma_start(wqk[:], w_qk_t.rearrange("(c p) n -> p c n", p=P)).then_inc(ld_wa.sem, 16)
            sp.dma_start(wv[:], w_v_t.rearrange("(c p) n -> p c n", p=P)).then_inc(ld_wa.sem, 16)
            sp.dma_start(wo[:], w_o_t.rearrange("(c p) n -> p c n", p=P)).then_inc(ld_wa.sem, 16)
            with sp.Fori(1, PAIRS // 2) as k:
                for u in range(2):
                    sp.wait_ge(ld_x[u].sem, ld_x[u].at(k - 1))
                    load_x(2 * k + u, u)
            sp.dma_start(rows_id[:], row_ids).then_inc(ld_small.sem, 16)
            for dst, src in ((gnb, gn_b), (gnw, gn_w), (rbias, router_b)):
                sp.dma_start(dst[:], src.rearrange("(a n) -> a n", a=1).to_broadcast([P, dst.shape[1]])
                             ).then_inc(ld_small.sem, 16)
            for row, at in ((0, X_HEADS), (32, 0)):
                sp.dma_start(gate_bias[row:row + X_HEADS], gate_b[at:at + X_HEADS].rearrange("(h a) -> h a", a=1)
                             ).then_inc(ld_small.sem, 16)
            sp.dma_start(rw[:], router_w.rearrange("(c p) n -> p c n", p=P)).then_inc(ld_small.sem, 16)
            sp.dma_start(b2_sb[:], b2).then_inc(ld_small.sem, 16)
            sp.dma_start(b1_sb[:], b1).then_inc(ld_b1.sem, 16)
            sp.dma_start(gw[:], gate_w_t.rearrange("(c p) n -> p c n", p=P)).then_inc(ld_small.sem, 16)

            load_w(sp, 0, 0)
            load_w(sp, 1, 1)
            sp.wait_ge(setup.sem, setup.at(0))
            sp.dma_start(out[TOKENS:OUT_ROWS, :].rearrange("(k p) n -> p k n", p=P),
                         pad[:, :, 0:DIM]).then_inc(trash_dma.sem, 16)

            def cross(i, u, on, half_):
                if on(0):
                    if has(i - 2):
                        sp.wait_ge(gates.sem, gates.at(i - 2))
                        sp.wait_ge(scores.sem, scores.at(i - 2))
                        sp.wait_ge(v_mm.sem, v_mm.at(i - 2))
                    sp.dma_start(c_t[:, u], ctx_t[bass.ds(i, 1)].rearrange("a (c p) i -> p (a c) i", p=P)
                                 ).then_inc(ld_ct[u].sem, 16)
                    for r in range(4):
                        sp.dma_start(c_x[X_DH * r:X_DH * (r + 1), u, :, r],
                                     ctx_t[bass.ds(i, 1)].rearrange("a (c r p) i -> r p (a c) i", c=CH, r=4)[r]
                                     ).then_inc(ld_cx[u].sem, 16)
                if on(8):
                    sp.wait_ge(init_add.sem, init_add.at(i - 8))
                    sp.dma_start(out_v[:, bass.ds(i - 8, 1), :], o_init[:, u].rearrange("p (a d) -> p a d", a=1)
                                 ).then_inc(store[u].sem, 16)

            skewed(sp, SEQS, CROSS_LAGS, cross)

            sp.wait_ge(tiling.sem, tiling.at(0))

            def write_tail(e):
                row = sp.value_load(t_end[0:1, bass.ds(e, 1)], min_val=0, max_val=(EXPERTS - 1) * REGION + TOKENS)
                if has(e - 1):
                    sp.wait_ge(tail.sem, tail.at(e - 1))
                sp.dma_start(routed[bass.ds(row, ROWS), :].rearrange("(k p) n -> p k n", p=P), pad[:]
                             ).then_inc(tail.sem, 16)

            def load_rows(i, e, row):
                sp.wait_ge(tail.sem, tail.at(e))
                if has(i - 1):
                    sp.wait_ge(rows_t.sem, rows_t.at(i - 1))
                    sp.wait_ge(rows_meta.sem, rows_meta.at(i - 1))
                sp.dma_start(xt_rows[:], routed[bass.ds(row, ROWS), :].rearrange("(k p) n -> p k n", p=P)
                             ).then_inc(ld_rows.sem, 16)

            def expert(e, first, end, tail_follows):
                if tail_follows:
                    write_tail(e + 1)

                def load(i):
                    load_rows(i, e, nc.s_assert_within(
                        (i - first) * ROWS + e * REGION, 0, EXPERTS * REGION - ROWS,
                        skip_runtime_bounds_check_because="an expert's tiles lie in its region"))

                load(first)
                with sp.If(end > first + 1):
                    with sp.Fori(first + 1, end) as i:
                        load(i)

            def four_experts(four, last):
                at = tile_bounds(sp, four)
                if isinstance(four, int) and four == 0:
                    for u in range(2):
                        sp.wait_ge(scatter[u].sem, scatter[u].at(SEQS // 2 - 1))
                for u in range(4):
                    expert(4 * four + u, at[u], at[u + 1], tail_follows=not (last and u == 3))

            write_tail(0)
            four_experts(0, False)
            with sp.Fori(1, EXPERTS // 4 - 1) as four:
                four_experts(four, False)
            four_experts(EXPERTS // 4 - 1, True)
            total = sp.value_load(t_first[0:1, EXPERTS:EXPERTS + 1], min_val=EXPERTS, max_val=MAX_TILES)
            load_rows(total, EXPERTS - 1, 0)
            sp.wait_ge(trash_dma.sem, trash_dma.at(0))
            for u in range(2):
                sp.wait_ge(store[u].sem, store[u].at(SEQS // 2 - 1))

        @block.gpsimd
        def _(pool):
            pool.memset(half[:], -0.5).then_inc(cst_ready.sem, 1)
            pool.memset(eps[:], EPS).then_inc(cst_ready.sem, 1)
            pool.wait_ge(cst_ready.sem, cst_ready.at(0))

            def attention(i, u, on, half_):
                if on(0):
                    pool.wait_ge(a_stats.sem, a_stats.at(i))
                    if has(i - 1):
                        pool.wait_ge(a_ready.sem, a_ready.at(i - 1))
                    pool.tensor_tensor(a_var[:], a_mv[:, :, 1], eps[:, 0:2], ALU.add).then_inc(a_norm.sem, 1)
                    pool.wait_ge(a_norm.sem, a_norm.at(i, 1))
                    pool.tensor_tensor(a_rstd[:], a_var[:], half[:, 0:2], ALU.pow).then_inc(a_norm.sem, 1)

            skewed(pool, PAIRS, 4, attention)
            pool.wait_ge(setup.sem, setup.at(0))

            def cross(i, u, on, half_):
                v = (u + 1) % 2
                if on(0) or on(4):
                    pool.wait_ge(variances.sem, variances.at(i))
                    if has(i - 1):
                        pool.wait_ge(mean_r.sem, mean_r.at(i - 1))
                    if on(1):
                        pool.wait_ge(ln2_q.sem, ln2_q.at(i - 1))
                    if on(5):
                        pool.wait_ge(ln3_x.sem, ln3_x.at(i - 5))
                    pool.tensor_tensor(n_rstd[:], n_var[:], n_half[:], ALU.pow).then_inc(rsqrt.sem, 1)
                if on(3):
                    pool.wait_ge(rsqrt.sem, rsqrt.at(i))
                    if has(i - 4):
                        pool.wait_ge(h_scale.sem, h_scale.at(i - 4))
                    pool.tensor_tensor(h_fw[:].rearrange("p (h d) -> p h d", d=X_DH),
                                       n_rstd[:, 2:].rearrange("p (h a) -> p h a", a=1)
                                       .to_broadcast([P, X_HEADS, X_DH]),
                                       gnw[:].rearrange("p (h d) -> p h d", d=X_DH), ALU.mult
                                       ).then_inc(h_factor.sem, 1)
                if on(1):
                    pool.wait_ge(ln2_q.sem, ln2_q.at(i - 1))
                    pool.tensor_tensor(seq(i - 1), seq(i - 1), gnb[:], ALU.add).then_inc(bias_in.sem, 1)
                if on(3):
                    pool.wait_ge(h_scale.sem, h_scale.at(i - 3))
                    pool.wait_ge(bias_in.sem, bias_in.at(i - 3))
                    pool.tensor_tensor(seq(i - 3), seq(i - 3), h_n[:], ALU.add).then_inc(h_out.sem, 1)
                if on(5):
                    pool.wait_ge(dest.sem, dest.at(i - 5))
                    pool.tensor_tensor(pay[:, v, DIM:C_ROW], r_me[:], r_i[:].to_broadcast([P, EXPERTS]), ALU.mult
                                       ).then_inc(weights.sem, 1)
                    pool.drain()
                    for k in range(TOP_K):
                        pool.indirect_dma_start(routed, bass.IndirectOffsetOnAxis(ap=r_dst[:, v, k:k + 1], axis=0),
                                                pay[:, v, :], None).then_inc(scatter[v].sem, 16)

            skewed(pool, SEQS, CROSS_LAGS, cross)

            for u in range(2):
                pool.wait_ge(store[u].sem, store[u].at(SEQS // 2 - 1))
            pool.wait_ge(trash_dma.sem, trash_dma.at(0))

            pool.wait_ge(tiling.sem, tiling.at(0))
            total = pool.value_load(t_first[0:1, EXPERTS:EXPERTS + 1], min_val=EXPERTS, max_val=MAX_TILES)

            def add(i):
                pool.wait_ge(y_out.sem, y_out.at(i))
                pool.wait_ge(rows_meta.sem, rows_meta.at(i))
                pool.tensor_copy(e_idx[:], e_id[:, bass.ds(i % 2, 1)].rearrange("p a k -> p (a k)")
                                 ).then_inc(idx_out.sem, 1)
                pool.drain()
                for k in range(BLOCKS):
                    pool.indirect_dma_start(out, bass.IndirectOffsetOnAxis(ap=e_idx[:, k:k + 1], axis=0),
                                            e_y[k][:], None, compute_op=ALU.add).then_inc(added.sem, 16)
                pool.wait_ge(added.sem, added.at(i))

            add(0)
            with pool.Fori(1, total) as i:
                add(i)

        @block.vector
        def _(dve):
            dve.memset(x_am[:], 0.0).then_inc(setup.sem, 1)
            dve.memset(x_hl[:].bitcast(F32), 0.0).then_inc(setup.sem, 1)
            dve.memset(v_c[:], 1.0 / TAU).then_inc(setup.sem, 1)
            dve.memset(c_x[:], 0.0).then_inc(setup.sem, 1)
            dve.memset(pay[:], 0.0)
            dve.memset(pad[:], 0.0)
            dve.memset(ones_bf[:], 1.0)
            dve.memset(t_ones[:], 1.0)
            dve.memset(t_scan[:], 0.0)
            dve.memset(n_half[:], -0.5)
            dve.memset(n_var[:], 1.0)
            dve.memset(n_mv[:], 1.0)
            dve.memset(gw_t[:], 0.0)
            dve.wait_ge(ld_cst.sem, ld_cst.at(0))
            dve.tensor_copy(ident_r[:], ident)
            dve.tensor_copy(causal_r[:], cst[:, C_CAUSAL:C_CAUSAL + P].rearrange("p (a j) -> p a j", a=1)
                            .to_broadcast([P, 4, P]))
            dve.tensor_copy(tri_before[:], cst[:, C_TRIX:C_TRIX + P])
            dve.tensor_copy(sel_r[:].rearrange("k (h j) -> k h j", j=P), cst[0:HL_ROWS, C_SEL:C_SEL + 2 * X_HEADS]
                            .rearrange("k (h a) -> k h a", a=1).to_broadcast([HL_ROWS, 2 * X_HEADS, P]))

            def attention(i, u, on, half_):
                if on(4):
                    dve.wait_ge(a_pvh.sem, a_pvh.at(i - 4))
                    if has(i - 5):
                        dve.wait_ge(a_o.sem, a_o.at(i - 5))
                    dve.tensor_tensor(a_zl[:].rearrange("p c b i -> p (c b i)"), ps_z2[:, :],
                                      a_zh[:].bitcast(F32).rearrange("p c b i -> p (c b i)"), ALU.subtract
                                      ).then_inc(a_pvc.sem, 1)
                if on(3):
                    dve.wait_ge(a_zz.sem, a_zz.at(i - 3))
                    if has(i - 4):
                        dve.wait_ge(a_e.sem, a_e.at(i - 4))
                    dve.scalar_tensor_tensor(a_z[:], ps_z[:, :].rearrange("p (k j) -> p k j", k=4), A_DH ** -0.5,
                                             block_mask.rearrange("p (a j) -> p a j", a=1).to_broadcast([P, 4, P]),
                                             ALU.mult, ALU.add).then_inc(a_zm.sem, 1)
                    dve.wait_ge(a_zm.sem, a_zm.at(i - 3, 1))
                    dve.tensor_reduce(a_max[:], a_z[:], AX.X, ALU.max).then_inc(a_zm.sem, 1)
                    dve.wait_ge(a_zm.sem, a_zm.at(i - 3, 2))
                    dve.tensor_scalar(a_neg[:], a_max[:], -1.0, None, ALU.mult).then_inc(a_zm.sem, 1)
                if on(1):
                    dve.wait_ge(a_norm.sem, a_norm.at(i - 1))
                    if has(i - 2):
                        dve.wait_ge(a_t.sem, a_t.at(i - 2))
                    for b in range(2):
                        dve.tensor_scalar(a_xn[:, b], res[:, bass.ds(2 * (i - 1) + b, 1), :].rearrange(
                            "p a d -> p (a d)"), a_mv[:, b, 0:1], a_rstd[:, b:b + 1], ALU.subtract, ALU.mult
                            ).then_inc(a_ready.sem, 1)
                if on(3):
                    dve.wait_ge(a_e.sem, a_e.at(i - 3))
                    if has(i - 4):
                        dve.wait_ge(a_pv.sem, a_pv.at(i - 4))
                    dve.reciprocal(a_inv[:], a_sum[:]).then_inc(a_sc.sem, 1)
                    dve.wait_ge(a_sc.sem, a_sc.at(i - 3, 1))
                    dve.tensor_tensor(a_pn[:], a_p[:], a_inv[:].rearrange("p (k a) -> p k a", a=1)
                                      .to_broadcast([P, 4, P]), ALU.mult).then_inc(a_sc.sem, 1)
                if on(4):
                    dve.wait_ge(a_o.sem, a_o.at(i - 4))
                    pair = res[:, bass.ds(2 * (i - 4), 2), :]
                    dve.tensor_tensor(pair, pair, ps_o[:, :].rearrange("p (b d) -> p b d", b=2),
                                      ALU.add).then_inc(a_res.sem, 1)
                if on(0):
                    dve.wait_ge(ld_x[u].sem, ld_x[u].at(half_(0)))
                    if has(i - 1):
                        dve.wait_ge(a_norm.sem, a_norm.at(i - 1))
                        dve.wait_ge(a_ready.sem, a_ready.at(i - 1))
                    for b in range(2):
                        dve.bn_stats(a_stat[:, b], res[:, 2 * i + b, :] if isinstance(i, int) else
                                     res[:, bass.ds(2 * i + b, 1), :].rearrange("p a d -> p (a d)")
                                     ).then_inc(a_stats.sem, 1)
                    dve.drain()
                    for b in range(2):
                        dve.bn_aggr(a_mv[:, b], a_stat[:, b]).then_inc(a_stats.sem, 1)
                if on(1):
                    dve.wait_ge(a_th.sem, a_th.at(i - 1))
                    if has(i - 2):
                        dve.wait_ge(a_v.sem, a_v.at(i - 2))
                    dve.tensor_tensor(a_xl[:].rearrange("p c b i -> p (c b i)"), ps_t[:, :],
                                      a_xh[:].bitcast(F32).rearrange("p c b i -> p (c b i)"), ALU.subtract
                                      ).then_inc(a_tc.sem, 1)
                if isinstance(i, int) and i in (1, 2):
                    split_wa(i - 1)

            def split_wa(i):
                for k in ((0, 1) if i == 0 else (2,)):
                    dve.wait_ge(wa_hi.sem, wa_hi.at(0, k + 1))
                    w, hi, lo = ((wqk, wqk_hi, wqk_lo), (wv, wv_hi, wv_lo), (wo, wo_hi, wo_lo))[k]
                    dve.tensor_tensor(lo[:], w[:], hi[:].bitcast(F32), ALU.subtract).then_inc(wa_lo.sem, 1)

            skewed(dve, PAIRS, 4, attention)

            def split_w(e, u, quarter):
                at = slice(quarter * WN // 4, (quarter + 1) * WN // 4)
                dve.wait_ge(w_hi_s.sem, w_hi_s.at(e, quarter + 1))
                dve.tensor_tensor(w_lo[u][:, at], w_in[:, u % 2, at], w_hi[u][:, at].bitcast(F32), ALU.subtract
                                  ).then_inc(w_lo_s.sem, 1)

            dve.wait_ge(ld_small.sem, ld_small.at(0))
            dve.tensor_scalar(minus_bias[:], gate_bias[0:X_HEADS], -1.0, None, ALU.mult)
            dve.drain()
            dve.tensor_copy(pad[:, :, C_ROW].bitcast(I32), rows_id[:, SEQS:SEQS + BLOCKS]).then_inc(setup.sem, 1)
            dve.drain().then_inc(setup.sem, 1)
            for column, at in ((0, X_HEADS), (32, 0)):
                heads_, out_ = slice(at, at + X_HEADS), slice(column, column + X_HEADS)
                dve.tensor_copy(gw_t[:, 0:CH, out_], gw[:, 0:CH, heads_])
                dve.tensor_tensor(gw_t[:, CH:, out_], gw[:, CH:2 * CH, heads_], gw[:, 2 * CH:3 * CH, heads_], ALU.add)
            dve.drain().then_inc(setup.sem, 1)
            dve.tensor_copy(r_base[:], cst[:, C_BASE:C_BASE + EXPERTS]).then_inc(setup.sem, 1)
            dve.drain()

            def count_tiles():
                dve.tensor_tensor(t_cnt[:], r_base[:], cst[:, C_BASE:C_BASE + EXPERTS], ALU.subtract)
                dve.tensor_copy(t_end[:], r_base[:])
                dve.drain()
                dve.tensor_tensor(t_cmp[:], t_cnt[:].rearrange("p (e a) -> p e a", a=1)
                                  .to_broadcast([P, EXPERTS, 16]),
                                  cst[:, C_THR:C_SEL].rearrange("p (e k) -> p e k", k=16), ALU.is_gt)
                dve.drain()
                dve.tensor_reduce(t_num[:], t_cmp[:], AX.X, ALU.add)
                dve.drain()
                dve.tensor_scalar(t_num[:], t_num[:], 1.0, None, ALU.add)
                dve.drain()
                dve.tensor_tensor_scan(t_scan[:, 1:EXPERTS + 1], t_ones[:], t_num[:], 0.0, ALU.mult, ALU.add)
                dve.drain()
                dve.tensor_copy(t_first[:], t_scan[:]).then_inc(tiling.sem, 1)

            def cross(i, u, on, half_):
                v = (u + 1) % 2
                norms = on(0) or on(4)
                if on(0):
                    dve.bn_stats(n_stat[:, 0], seq(i))
                if on(4):
                    dve.wait_ge(h_out.sem, h_out.at(i - 4))
                    dve.bn_stats(n_stat[:, 1], seq(i - 4))
                if on(5):
                    dve.wait_ge(logits.sem, logits.at(i - 5))
                    if has(i - 6):
                        dve.wait_ge(weights.sem, weights.at(i - 6))
                    dve.tensor_tensor(r_lg[:], ps_lg, rbias[:], ALU.add).then_inc(logits_b.sem, 1)
                if on(3):
                    dve.wait_ge(expm.sem, expm.at(i - 3))
                    dve.tensor_tensor(h_max[:], h_abs[:], x_em[:], ALU.max)
                    dve.wait_ge(h_square.sem, h_square.at(i - 3))
                    dve.tensor_reduce(h_ss[:], h_sq[:], AX.X, ALU.add)
                dve.drain()
                if on(0):
                    dve.bn_aggr(n_mv[:, 0], n_stat[:, 0])
                if on(4):
                    dve.bn_aggr(n_mv[:, 1], n_stat[:, 1])
                if on(3):
                    dve.tensor_scalar(h_den[:], h_max[:], 1e-6, None, ALU.add)
                dve.drain()
                if norms:
                    if has(i - 1):
                        dve.wait_ge(rsqrt.sem, rsqrt.at(i - 1))
                    dve.tensor_scalar(n_var[:, 0:2], n_mv[:, :, 1], EPS, None, ALU.add)
                if on(3):
                    dve.scalar_tensor_tensor(h_e2[:], h_den[:], EPS, h_den[:], ALU.mult, ALU.mult)
                dve.drain()
                if on(3):
                    dve.tensor_tensor(n_var[:, 2:], h_e2[:], h_ss[:], ALU.add)
                if norms:
                    dve.drain().then_inc(variances.sem, 1)
                if on(2):
                    if has(i - 3):
                        dve.wait_ge(heads.sem, heads.at(i - 3))
                    dve.wait_ge(scores.sem, scores.at(i - 2, 1))
                    dve.wait_ge(decay.sem, decay.at(i - 2, 1))
                    dve.tensor_tensor(x_c[:, 0:4], ps_s[:, 0:4], x_d[:, 0:4], ALU.mult).then_inc(weigh.sem, 1)
                if on(5):
                    dve.max(r_top[:], r_lg[:])
                    dve.drain()
                    dve.tensor_scalar(r_neg[:], r_top[:, 0:1], -1.0, None, ALU.mult)
                    dve.max_index(r_idx[:], r_top[:], r_lg[:]).then_inc(pick4.sem, 1)
                    dve.drain()
                if on(5):
                    dve.tensor_tensor(r_hot[:], iota16.rearrange("p (a e) -> p a e", a=1).to_broadcast(
                        [P, TOP_K, EXPERTS]), r_idx[:, 0:TOP_K].rearrange("p (k a) -> p k a", a=1).to_broadcast(
                        [P, TOP_K, EXPERTS]), ALU.is_equal)
                    dve.drain()
                    with nc.allow_low_precision(reason="zeros and ones"):
                        dve.tensor_reduce(r_maskb[:], r_hot[:].rearrange("p k e -> p e k"), AX.X, ALU.add
                                          ).then_inc(masks.sem, 1)
                if on(1):
                    dve.wait_ge(gates_ln.sem, gates_ln.at(i - 1))
                    dve.tensor_tensor_scan(x_ncs[32:40, :], x_relu[:], x_ln[:], 0.0, ALU.add, ALU.add
                                           ).then_inc(ncs.sem, 1)
                if on(2):
                    dve.wait_ge(scores.sem, scores.at(i - 2))
                    dve.wait_ge(decay.sem, decay.at(i - 2))
                    dve.tensor_tensor(x_c[:, 4:8], ps_s[:, 4:8], x_d[:, 4:8], ALU.mult).then_inc(weigh.sem, 1)
                if on(1):
                    dve.wait_ge(ncs.sem, ncs.at(i - 1))
                    dve.scalar_tensor_tensor(x_am[0:X_HEADS, :], ps_i, gate_bias[32:40], x_ncs[32:40, :],
                                             ALU.add, ALU.add).then_inc(a_read.sem, 1)
                if norms:
                    dve.wait_ge(rsqrt.sem, rsqrt.at(i))
                    dve.scalar_tensor_tensor(n_mr[:], n_mv[:, :, 0], -1.0, n_rstd[:, 0:2], ALU.mult, ALU.mult
                                             ).then_inc(mean_r.sem, 1)
                if on(1):
                    dve.wait_ge(a_read.sem, a_read.at(i - 1))
                    dve.tensor_tensor_scan(x_am[32:40, :], x_am[0:X_HEADS, :], x_am[0:X_HEADS, :],
                                           -3e38, ALU.max, ALU.max).then_inc(a_run.sem, 1)
                if on(5):
                    dve.wait_ge(rexp.sem, rexp.at(i - 5))
                    dve.wait_ge(masks.sem, masks.at(i - 5))
                    dve.tensor_tensor(r_me[:], r_e[:], r_maskb[:], ALU.mult)
                    dve.tensor_copy(pay[:, v, C_ROW:C_ROW + 1].bitcast(I32), rows_id[:, bass.ds(i - 5, 1)])
                if on(3):
                    dve.wait_ge(h_factor.sem, h_factor.at(i - 3))
                    if has(i - 4):
                        dve.wait_ge(h_out.sem, h_out.at(i - 4))
                    dve.tensor_tensor(h_n[:].rearrange("p (h d) -> p h d", d=X_DH), ps_h[v][:, :, 0:X_DH],
                                      h_fw[:].rearrange("p (h d) -> p h d", d=X_DH), ALU.mult
                                      ).then_inc(h_scale.sem, 1)
                if on(1):
                    dve.wait_ge(a_high.sem, a_high.at(i - 1))
                    dve.tensor_tensor(x_hl[64:104, v], x_am[:], x_hl[0:40, v].bitcast(F32), ALU.subtract
                                      ).then_inc(a_scan.sem, 1)
                    if has(i - 3):
                        dve.wait_ge(maxt.sem, maxt.at(i - 3))
                    dve.tensor_tensor(x_m[32:40, v], x_am[32:40, :], x_ncs[32:40, :], ALU.subtract
                                      ).then_inc(row_max.sem, 1)
                if on(7):
                    dve.wait_ge(init_mm.sem, init_mm.at(i - 7))
                    if on(1):
                        dve.wait_ge(v_tc.sem, v_tc.at(i - 1))
                    if has(i - 9):
                        dve.wait_ge(store[v].sem, store[v].at(half_(7) - 1))
                    dve.tensor_tensor(o_init[:, v], ps_init, seq(i - 7), ALU.add).then_inc(init_add.sem, 1)
                if on(5):
                    dve.drain()
                    dve.wait_ge(place.sem, place.at(i - 5))
                    dve.tensor_reduce(r_s[:], r_me[:], AX.X, ALU.add)
                    dve.tensor_tensor(r_pos[:], ps_pos, r_base[:], ALU.add)
                dve.drain()
                if on(5):
                    dve.reciprocal(r_i[:], r_s[:])
                    dve.tensor_tensor(r_base[:], r_base[:], ps_tot, ALU.add).then_inc(placed.sem, 1)
                    dve.tensor_tensor(r_dsel[:], r_hot[:], r_pos[:].rearrange("p (a e) -> p a e", a=1).to_broadcast(
                        [P, TOP_K, EXPERTS]), ALU.mult)
                dve.drain()
                if on(5):
                    with nc.allow_low_precision(reason="whole numbers"):
                        dve.tensor_reduce(r_dst[:, v], r_dsel[:], AX.X, ALU.add).then_inc(dest.sem, 1)
                dve.drain()
                if isinstance(i, int) and i < 8:
                    split_w(i // 4, i // 4, i % 4)
                if isinstance(i, int) and i == SEQS + 4:
                    count_tiles()

            skewed(dve, SEQS, CROSS_LAGS, cross)

            def meta(i):
                dve.wait_ge(ld_rows.sem, ld_rows.at(i))
                if has(i - 2):
                    dve.wait_ge(idx_out.sem, idx_out.at(i - 2))
                    dve.wait_ge(y_out.sem, y_out.at(i - 2))
                dve.tensor_copy(e_wt[:, bass.ds(i % 2, 1)].rearrange("p a k e -> p (a k) e"),
                                xt_rows[:, :, DIM:C_ROW])
                dve.tensor_copy(e_id[:, bass.ds(i % 2, 1)].rearrange("p a k -> p (a k)"),
                                xt_rows[:, :, C_ROW].bitcast(U32)).then_inc(rows_meta.sem, 1)

            def rows(i):
                dve.wait_ge(rows_hi.sem, rows_hi.at(i))
                dve.tensor_tensor(e_xl[:], ps_x, e_xh[:].bitcast(F32), ALU.subtract).then_inc(rows_lo.sem, 1)

            def tile(i, e, split=None):
                for m in range(HC):
                    if split and m < HC - 1:
                        split_w(*split, m)
                    if m == HC - 1:
                        meta(i + 1)
                    dve.wait_ge(gelu[m].sem, gelu[m].at(i))
                    if has(i - 1):
                        dve.wait_ge(down.sem, down.at(i - 1))
                    dve.tensor_tensor(e_hl[:, m], e_h[:, m], e_hh[:, m].bitcast(F32), ALU.subtract
                                      ).then_inc(h_lo[m].sem, 1)
                rows(i + 1)
                if split:
                    split_w(*split, 3)
                dve.wait_ge(down.sem, down.at(i))
                if has(i - 1):
                    dve.wait_ge(added.sem, added.at(i - 1))
                for k in range(BLOCKS):
                    dve.tensor_scalar(e_y[k][:], ps_y[k], e_wt[:, bass.ds(i % 2, 1), k, bass.ds(e, 1)].rearrange(
                        "p a b -> p (a b)"), None, ALU.mult).then_inc(y_out.sem, 1)

            def expert(e, u, first, end, splits):
                splits = splits and not (isinstance(e, int) and e == 0)
                tile(first, e, (e + 2, (u + 2) % 4) if splits else None)
                with dve.If(end > first + 1):
                    with dve.Fori(first + 1, end) as i:
                        tile(i, e)

            for quarter in range(4):
                split_w(2, 2, quarter)
            meta(0)
            rows(0)

            def four_experts(four, last):
                at = tile_bounds(dve, four)
                for u in range(4):
                    expert(4 * four + u, u, at[u], at[u + 1], splits=not last or u < 2)

            four_experts(0, False)
            with dve.Fori(1, EXPERTS // 4 - 1) as four:
                four_experts(four, False)
            four_experts(EXPERTS // 4 - 1, True)

        @block.scalar
        def _(act):
            act.preload_act_table_set("natural_log_exp_and_others")
            act.wait_ge(ld_wa.sem, ld_wa.at(0))
            for w, hi in ((wqk, wqk_hi), (wv, wv_hi), (wo, wo_hi)):
                act.copy(hi[:], w[:]).then_inc(wa_hi.sem, 1)

            def attention(i, u, on, half_):
                if on(3):
                    act.wait_ge(a_zm.sem, a_zm.at(i - 3))
                    if has(i - 4):
                        act.wait_ge(a_sc.sem, a_sc.at(i - 4))
                    for k in range(4):
                        act.activation(a_p[:, k], a_z[:, k], ACT.Exp, bias=a_neg[:, k:k + 1],
                                       accum_out=a_sum[:, k:k + 1]).then_inc(a_e.sem, 1)
                if on(2):
                    if has(i - 3):
                        act.wait_ge(a_zz.sem, a_zz.at(i - 3))
                    for b in range(2):
                        act.wait_ge(a_proj.sem, a_proj.at(i - 2, b + 1))
                        act.copy(a_qk[:, b], ps_qk[b][:, :]).then_inc(a_projc.sem, 1)
                    act.wait_ge(a_v.sem, a_v.at(i - 2))
                    if has(i - 4):
                        act.wait_ge(a_pv.sem, a_pv.at(i - 4))
                    act.copy(a_vt[:, u].rearrange("p c b i -> p (c b i)"), ps_av).then_inc(a_vc.sem, 1)
                if on(1):
                    act.wait_ge(a_t.sem, a_t.at(i - 1))
                    if has(i - 2):
                        act.wait_ge(a_v.sem, a_v.at(i - 2))
                    act.copy(a_xh[:].rearrange("p c b i -> p (c b i)"), ps_t[:, :]).then_inc(a_th.sem, 1)
                if on(3):
                    act.wait_ge(a_pv.sem, a_pv.at(i - 3))
                    if has(i - 4):
                        act.wait_ge(a_o.sem, a_o.at(i - 4))
                    act.copy(a_zh[:].rearrange("p c b i -> p (c b i)"), ps_z2[:, :]).then_inc(a_pvh.sem, 1)

            skewed(act, PAIRS, 4, attention)

            def split_w(e, u, half_of_e, quarters=range(4)):
                act.wait_ge(ld_w[u % 2].sem, ld_w[u % 2].at(half_of_e))
                for quarter in quarters:
                    at = slice(quarter * WN // 4, (quarter + 1) * WN // 4)
                    act.copy(w_hi[u][:, at], w_in[:, u % 2, at]).then_inc(w_hi_s.sem, 1)

            def refill(e, u):
                act.wait_ge(w_lo_s.sem, w_lo_s.at(e))
                load_w(act, e + 2, u % 2)

            act.wait_ge(setup.sem, setup.at(0))

            def cross(i, u, on, half_):
                v = (u + 1) % 2
                if on(3):
                    act.wait_ge(maxt.sem, maxt.at(i - 3))
                    if has(i - 4):
                        act.wait_ge(variances.sem, variances.at(i - 1))
                    act.activation(h_abs[:], ps_h[v][:, :, X_DH], ACT.Abs)
                    act.activation(x_em[:], ps_mt[v], ACT.Exp, scale=-1.0).then_inc(expm.sem, 1)
                    act.activation(h_sq[:], ps_h[v][:, :, 0:X_DH], ACT.Square, scale=X_DH ** -0.5
                                   ).then_inc(h_square.sem, 1)
                if on(1):
                    act.wait_ge(q_t.sem, q_t.at(i - 1))
                    if on(5):
                        act.wait_ge(rx_t.sem, rx_t.at(i - 5))
                    if has(i - 3):
                        act.wait_ge(scores.sem, scores.at(i - 3))
                        act.wait_ge(gates.sem, gates.at(i - 3))
                    act.copy(x_qt[:, v], ps_qt).then_inc(q_tc.sem, 1)
                if on(5):
                    act.wait_ge(rx_t.sem, rx_t.at(i - 5))
                    if has(i - 6):
                        act.wait_ge(logits.sem, logits.at(i - 6))
                    act.copy(r_xt[:], ps_xt).then_inc(rx_tc.sem, 1)
                if on(2):
                    for k in range(2):
                        act.wait_ge(args.sem, args.at(i - 2, k + 1))
                        if has(i - 3):
                            act.wait_ge(weigh.sem, weigh.at(i - 3, k + 1))
                        act.activation(x_d[:, 4 * k:4 * k + 4].rearrange("p h i -> p (h i)"), banks[2 + k], ACT.Exp
                                       ).then_inc(decay.sem, 1)
                if on(1):
                    act.wait_ge(gates.sem, gates.at(i - 1))
                    if has(i - 2):
                        act.wait_ge(ncs.sem, ncs.at(i - 2))
                    act.activation(x_relu[:], ps_f, ACT.Relu, bias=minus_bias[:], scale=-1.0)
                    act.activation(x_abs[:], ps_f, ACT.Abs, bias=gate_bias[0:X_HEADS])
                    act.drain()
                    act.activation(x_ea[:], x_abs[:], ACT.Exp, scale=-1.0)
                    act.drain()
                    act.activation(x_ln[:], x_ea[:], ACT.Ln, bias=1.0).then_inc(gates_ln.sem, 1)
                    act.wait_ge(v_mm.sem, v_mm.at(i - 1))
                    if has(i - 3):
                        act.wait_ge(heads.sem, heads.at(i - 3))
                    act.mul(v_c[:, v, :, 0:X_DH], ps_v.rearrange("p (h d) -> p h d", d=X_DH), 1.0 / TAU
                            ).then_inc(v_tc.sem, 1)
                if on(5):
                    act.wait_ge(pick4.sem, pick4.at(i - 5))
                    act.activation(r_e[:], r_lg[:], ACT.Exp, bias=r_neg[:]).then_inc(rexp.sem, 1)
                if on(6):
                    act.wait_ge(w_t.sem, w_t.at(i - 6))
                    if has(i - 7):
                        act.wait_ge(init_mm.sem, init_mm.at(i - 7))
                    act.copy(r_ct[:], ps_ct).then_inc(w_tc.sem, 1)
                if on(1):
                    act.wait_ge(a_run.sem, a_run.at(i - 1))
                    if has(i - 3):
                        act.wait_ge(args.sem, args.at(i - 3))
                    act.copy(x_hl[0:40, v], x_am[:]).then_inc(a_high.sem, 1)
                if on(0):
                    act.wait_ge(mean_r.sem, mean_r.at(i))
                    if has(i - 1):
                        act.wait_ge(q_t.sem, q_t.at(i - 1))
                    act.activation(x_q[:], seq(i), ACT.Identity, bias=n_mr[:, 0:1], scale=n_rstd[:, 0:1]
                                   ).then_inc(ln2_q.sem, 1)
                if on(4):
                    act.wait_ge(mean_r.sem, mean_r.at(i))
                    if has(i - 6):
                        act.wait_ge(scatter[u].sem, scatter[u].at(half_(4) - 1))
                    act.activation(pay[:, u, 0:DIM], seq(i - 4), ACT.Identity, bias=n_mr[:, 1:2], scale=n_rstd[:, 1:2]
                                   ).then_inc(ln3_x.sem, 1)
                if isinstance(i, int) and i < 8:
                    split_w(i // 4, i // 4, 0, [i % 4])
                if isinstance(i, int) and i in (6, 9):
                    refill(i // 9, i // 9)

            skewed(act, SEQS, CROSS_LAGS, cross)

            def rows(i):
                act.wait_ge(rows_t.sem, rows_t.at(i))
                if has(i - 1):
                    act.wait_ge(up[HC - 1].sem, up[HC - 1].at(i - 1))
                act.copy(e_xh[:], ps_x).then_inc(rows_hi.sem, 1)

            def tile(i):
                for m in range(HC):
                    act.wait_ge(up[m].sem, up[m].at(i))
                    if has(i - 1):
                        act.wait_ge(h_lo[m].sem, h_lo[m].at(i - 1))
                        act.wait_ge(down.sem, down.at(i - 1))
                    act.activation(e_h[:, m], ps_hid[m], ACT.Gelu, bias=e_b1[:, m:m + 1])
                    act.activation(e_hh[:, m], ps_hid[m], ACT.Gelu, bias=e_b1[:, m:m + 1]
                                   ).then_inc(gelu[m].sem, 1)
                rows(i + 1)

            def expert(e, u, half_, first, end, splits, loads):
                if splits and not (isinstance(e, int) and e == 0):
                    split_w(e + 2, (u + 2) % 4, half_ + 1)
                act.drain()
                act.copy(e_b1[:], b1_sb[:, bass.ds(e, 1)].rearrange("p a m -> p (a m)"))
                act.drain()
                tile(first)
                if loads:
                    refill(e + 2, u)
                with act.If(end > first + 1):
                    with act.Fori(first + 1, end) as i:
                        tile(i)

            act.wait_ge(ld_b1.sem, ld_b1.at(0))
            act.wait_ge(init_add.sem, init_add.at(SEQS - 1))
            split_w(2, 2, 1)
            act.wait_ge(tiling.sem, tiling.at(0))
            rows(0)

            def four_experts(four, last):
                at = tile_bounds(act, four)
                for u in range(4):
                    expert(4 * four + u, u, 2 * four + u // 2, at[u], at[u + 1], splits=not last or u < 2,
                           loads=not last)

            four_experts(0, False)
            with act.Fori(1, EXPERTS // 4 - 1) as four:
                four_experts(four, False)
            four_experts(EXPERTS // 4 - 1, True)

        @block.tensor
        def _(pe):
            pe.wait_ge(ld_cst.sem, ld_cst.at(0))

            def products(out_, pairs, first, last):
                todo = [p for (ah, al), (bh, bl) in pairs for p in ((ah, bh), (ah, bl), (al, bh))]
                for n, (a, b) in enumerate(todo):
                    mm = pe.matmul(out_, a, b, start=(first and n == 0), stop=(last and n == len(todo) - 1))
                return mm

            def attention(i, u, on, half_):
                if on(3):
                    pe.wait_ge(a_projc.sem, a_projc.at(i - 3))
                    if has(i - 4):
                        pe.wait_ge(a_zm.sem, a_zm.at(i - 4))
                    for b in range(2):
                        for c in range(CH):
                            mm = pe.matmul(ps_z[:, (2 * b + c) * P:(2 * b + c + 1) * P],
                                           a_qk[:, b, DIM + c * P:DIM + (c + 1) * P],
                                           a_qk[:, b, c * P:(c + 1) * P], start=True, stop=True)
                    mm.then_inc(a_zz.sem, 1)
                if on(2):
                    pe.wait_ge(a_tc.sem, a_tc.at(i - 2))
                    if isinstance(i, int) and i == 2:
                        pe.wait_ge(wa_lo.sem, wa_lo.at(0, 1))
                    for b in range(2):
                        if has(i - 3):
                            pe.wait_ge(a_projc.sem, a_projc.at(i - 3, b + 1))
                        products(ps_qk[b][:, :], [((a_xh[:, c, b], a_xl[:, c, b]), (wqk_hi[:, c], wqk_lo[:, c]))
                                                  for c in range(CH)], True, True).then_inc(a_proj.sem, 1)
                if on(4):
                    pe.wait_ge(a_pvc.sem, a_pvc.at(i - 4))
                    if has(i - 5):
                        pe.wait_ge(a_res.sem, a_res.at(i - 5))
                    if isinstance(i, int) and i == 4:
                        pe.wait_ge(wa_lo.sem, wa_lo.at(0))
                    for b in range(2):
                        mm = products(ps_o[:, b * DIM:(b + 1) * DIM],
                                      [((a_zh[:, c, b], a_zl[:, c, b]), (wo_hi[:, c], wo_lo[:, c]))
                                       for c in range(CH)], True, True)
                    mm.then_inc(a_o.sem, 1)
                if on(2):
                    if has(i - 3):
                        pe.wait_ge(a_vc.sem, a_vc.at(i - 3))
                    if isinstance(i, int) and i == 2:
                        pe.wait_ge(wa_lo.sem, wa_lo.at(0, 2))
                    for m in range(CH):
                        at = slice(m * P, (m + 1) * P)
                        mm = products(ps_av[:, m * 2 * P:(m + 1) * 2 * P], [
                            ((wv_hi[:, c, at], wv_lo[:, c, at]), (a_xh[:, c].rearrange("p b i -> p (b i)"),
                                                                  a_xl[:, c].rearrange("p b i -> p (b i)")))
                            for c in range(CH)], True, True)
                    mm.then_inc(a_v.sem, 1)
                if on(1):
                    pe.wait_ge(a_ready.sem, a_ready.at(i - 1))
                    if has(i - 2):
                        pe.wait_ge(a_tc.sem, a_tc.at(i - 2))
                    for c in range(CH):
                        for b in range(2):
                            mm = pe.transpose(ps_t[:, (2 * c + b) * P:(2 * c + b + 1) * P],
                                              a_xn[:, b, c * P:(c + 1) * P], ident)
                    mm.then_inc(a_t.sem, 1)
                if on(3):
                    pe.wait_ge(a_sc.sem, a_sc.at(i - 3))
                    pe.wait_ge(a_vc.sem, a_vc.at(i - 3))
                    if has(i - 4):
                        pe.wait_ge(a_pvc.sem, a_pvc.at(i - 4))
                    for c in range(CH):
                        for b in range(2):
                            mm = pe.matmul(ps_z2[:, (2 * c + b) * P:(2 * c + b + 1) * P], a_pn[:, 2 * b + c],
                                           a_vt[:, (u + 1) % 2, c, b], start=True, stop=True)
                    mm.then_inc(a_pv.sem, 1)

            skewed(pe, PAIRS, 4, attention)
            pe.wait_ge(setup.sem, setup.at(0))
            pe.wait_ge(a_res.sem, a_res.at(PAIRS - 1))
            pe.wait_ge(a_pvc.sem, a_pvc.at(PAIRS - 1))

            def cross(i, u, on, half_):
                v = (u + 1) % 2
                if on(1):
                    pe.wait_ge(ln2_q.sem, ln2_q.at(i - 1))
                    if has(i - 2):
                        pe.wait_ge(v_tc.sem, v_tc.at(i - 2))
                    if on(8):
                        pe.wait_ge(init_add.sem, init_add.at(i - 8))
                    for c in range(CH):
                        mm = pe.transpose(ps_qt[:, c], x_q[:, c * P:(c + 1) * P], ident)
                    mm.then_inc(q_t.sem, 1)
                if on(5):
                    pe.wait_ge(ln3_x.sem, ln3_x.at(i - 5))
                    if on(8):
                        pe.wait_ge(init_add.sem, init_add.at(i - 8))
                    for c in range(CH):
                        mm = pe.transpose(ps_xt[:, c], pay[:, v, c * P:(c + 1) * P], ident)
                    mm.then_inc(rx_t.sem, 1)

                def decay_args(k):
                    pe.wait_ge(a_scan.sem, a_scan.at(i - 2))
                    if has(i - 3):
                        pe.wait_ge(decay.sem, decay.at(i - 3, k + 1))
                    pe.matmul(ps_arg[k], ident_r[:], causal_r[:].rearrange("p h i -> p (h i)"),
                              start=True, stop=False)
                    pe.matmul(ps_arg[k], x_hl[:, u], sel_a[:, k * 4 * P:(k + 1) * 4 * P], start=False, stop=False)
                    for h in range(4):
                        mm = pe.matmul(ps_arg[k][:, h * P:(h + 1) * P], sel_max[:, 4 * k + h], x_hl[:, u],
                                       start=False, stop=(h == 3))
                    mm.then_inc(args.sem, 1)

                if on(2):
                    decay_args(0)
                if on(5):
                    pe.wait_ge(rx_tc.sem, rx_tc.at(i - 5))
                    if on(6):
                        pe.wait_ge(placed.sem, placed.at(i - 6))
                    for c in range(CH):
                        mm = pe.matmul(ps_lg, r_xt[:, c], rw[:, c], start=(c == 0), stop=(c == 1))
                    mm.then_inc(logits.sem, 1)
                if on(2):
                    decay_args(1)
                if on(1):
                    pe.wait_ge(q_tc.sem, q_tc.at(i - 1))
                    pe.wait_ge(ld_ct[v].sem, ld_ct[v].at(half_(1)))
                    if has(i - 2):
                        pe.wait_ge(a_read.sem, a_read.at(i - 2))
                    if on(5):
                        pe.wait_ge(logits_b.sem, logits_b.at(i - 5))
                    for n, a in enumerate([x_qt[:, v, c] for c in range(CH)] + [c_t[:, v, c] for c in range(CH)]):
                        mm = pe.matmul(ps_gates, gw_t[:, n], a, start=(n == 0), stop=(n == 3))
                    mm.then_inc(gates.sem, 1)
                if on(7):
                    pe.wait_ge(w_tc.sem, w_tc.at(i - 7))
                    if on(8):
                        pe.wait_ge(init_add.sem, init_add.at(i - 8))
                    if on(5):
                        pe.wait_ge(rx_tc.sem, rx_tc.at(i - 5))
                    pe.matmul(ps_init, r_ct[:], b2_sb[:], start=True, stop=True).then_inc(init_mm.sem, 1)
                if on(1):
                    if on(5):
                        pe.wait_ge(rx_tc.sem, rx_tc.at(i - 5))
                    for c in range(CH):
                        mm = pe.matmul(ps_v[:, c * P:(c + 1) * P], c_t[:, v, c], centre, start=True, stop=True)
                    mm.then_inc(v_mm.sem, 1)

                def heads_and_scores(n):
                    if on(2):
                        pe.wait_ge(weigh.sem, weigh.at(i - 2, n // 2 + 1))
                    if on(1):
                        if has(i - 2):
                            pe.wait_ge(weigh.sem, weigh.at(i - 2, n // 2 + 1))
                        pe.wait_ge(ld_cx[v].sem, ld_cx[v].at(half_(1)))
                    for h in (2 * n, 2 * n + 1):
                        if on(2):
                            mm = pe.matmul(ps_h[u][:, h], x_c[:, h], v_c[:, u, h], start=True, stop=True)
                            if h == X_HEADS - 1:
                                mm.then_inc(heads.sem, 1)
                        if on(1):
                            mm = pe.matmul(ps_s[:, h], c_x[:, v, h // 4, h % 4], x_qt[:, v, h // 4],
                                           start=True, stop=True)
                            if h % 4 == 3:
                                mm.then_inc(scores.sem, 1)

                if on(2):
                    pe.wait_ge(v_tc.sem, v_tc.at(i - 2))
                    if has(i - 4):
                        pe.wait_ge(h_scale.sem, h_scale.at(i - 4))
                heads_and_scores(0)
                if on(6):
                    pe.wait_ge(weights.sem, weights.at(i - 6))
                    if on(5):
                        pe.wait_ge(logits_b.sem, logits_b.at(i - 5))
                    if on(1):
                        pe.wait_ge(gates_ln.sem, gates_ln.at(i - 1))
                    pe.transpose(ps_ct, pay[:, u, DIM:C_ROW], ident).then_inc(w_t.sem, 1)
                if on(2):
                    pe.wait_ge(row_max.sem, row_max.at(i - 2))
                heads_and_scores(1)
                heads_and_scores(2)
                if on(5):
                    pe.wait_ge(masks.sem, masks.at(i - 5))
                    if on(1):
                        pe.wait_ge(a_read.sem, a_read.at(i - 1))
                    else:
                        pe.wait_ge(logits_b.sem, logits_b.at(i - 5))
                    if on(6):
                        pe.wait_ge(w_tc.sem, w_tc.at(i - 6))
                    pe.matmul(ps_pos, tri_before[:], r_maskb[:], start=True, stop=True)
                    pe.matmul(ps_tot, ones_bf[:], r_maskb[:], start=True, stop=True).then_inc(place.sem, 1)
                heads_and_scores(3)
                if on(2):
                    pe.transpose(ps_mt[u], x_m[32:40, u], cst[32:40, C_ID + 32:C_ID + 40]).then_inc(maxt.sem, 1)

            skewed(pe, SEQS, CROSS_LAGS, cross)

            def turn(i):
                pe.wait_ge(ld_rows.sem, ld_rows.at(i))
                if has(i - 1):
                    pe.wait_ge(rows_lo.sem, rows_lo.at(i - 1))
                for c in range(CH):
                    for k in range(BLOCKS):
                        mm = pe.transpose(ps_x[:, c, k * P:(k + 1) * P], xt_rows[:, k, c * P:(c + 1) * P], ident)
                mm.then_inc(rows_t.sem, 1)

            def tile(i, e, u):
                def w_up(c, m):
                    at = slice(c * HID + m * P, c * HID + (m + 1) * P)
                    return w_hi[u][:, at], w_lo[u][:, at]

                def w_down(m):
                    at = slice(W1N + m * DIM, W1N + (m + 1) * DIM)
                    return w_hi[u][:, at], w_lo[u][:, at]

                def up_(m):
                    if has(i - 1):
                        pe.wait_ge(gelu[m].sem, gelu[m].at(i - 1))
                    products(ps_hid[m], [(w_up(c, m), (e_xh[:, c], e_xl[:, c])) for c in range(CH)],
                             True, True).then_inc(up[m].sem, 1)

                def down_(m):
                    pe.wait_ge(h_lo[m].sem, h_lo[m].at(i))
                    for k in range(BLOCKS):
                        at = slice(k * P, (k + 1) * P)
                        mm = products(ps_y[k], [((e_hh[:, m, at], e_hl[:, m, at]), w_down(m))],
                                      m == 0, m == HC - 1)
                    return mm

                pe.wait_ge(w_lo_s.sem, w_lo_s.at(e))
                pe.wait_ge(rows_lo.sem, rows_lo.at(i))
                for m in range(HC):
                    up_(m)
                turn(i + 1)
                if has(i - 1):
                    pe.wait_ge(y_out.sem, y_out.at(i - 1))
                for m in range(HC - 1):
                    down_(m)
                down_(HC - 1).then_inc(down.sem, 1)

            def expert(e, u, first, end):
                tile(first, e, u)
                with pe.If(end > first + 1):
                    with pe.Fori(first + 1, end) as i:
                        tile(i, e, u)

            pe.wait_ge(tiling.sem, tiling.at(0))
            turn(0)

            def four_experts(four):
                at = tile_bounds(pe, four)
                for u in range(4):
                    expert(4 * four + u, u, at[u], at[u + 1])

            four_experts(0)
            with pe.Fori(1, EXPERTS // 4) as four:
                four_experts(four)


def kernel(x, ctx_1024, L0_attn_Wq, L0_attn_Wk, L0_attn_Wv, L0_attn_Wo, L0_xattn_Wi_w, L0_xattn_Wi_b,
           L0_xattn_Wf_w, L0_xattn_Wf_b, L0_xattn_gn_w, L0_xattn_gn_b, L0_ffn_router_w, L0_ffn_router_b,
           L0_ffn_w1, L0_ffn_b1, L0_ffn_w2, L0_ffn_b2):
    import concourse.bacc as bacc
    from concourse.bass_utils import run_bass_kernel_spmd

    consts, row_ids = shape_constants()
    arrays = {
        "x": x, "ctx_t": np.transpose(ctx_1024, (0, 2, 1)),
        "w_qk_t": np.concatenate([np.transpose(L0_attn_Wq), np.transpose(L0_attn_Wk)], axis=1),
        "w_v_t": np.transpose(L0_attn_Wv), "w_o_t": np.transpose(L0_attn_Wo),
        "gate_w_t": np.transpose(np.concatenate([L0_xattn_Wi_w, L0_xattn_Wf_w], axis=0)),
        "gate_b": np.concatenate([L0_xattn_Wi_b, L0_xattn_Wf_b]),
        "gn_w": L0_xattn_gn_w, "gn_b": L0_xattn_gn_b,
        "router_w": L0_ffn_router_w, "router_b": L0_ffn_router_b,
        "w1": L0_ffn_w1, "b1": np.transpose(np.reshape(L0_ffn_b1, (EXPERTS, HC, P)), (2, 0, 1)),
        "w2": L0_ffn_w2, "b2": L0_ffn_b2,
        "consts": consts, "row_ids": row_ids,
    }
    nc = bacc.Bacc("TRN2", target_bir_lowering=False, num_devices=1)
    ins, args = {}, []
    for name, a in arrays.items():
        ins[name] = np.ascontiguousarray(a)
        args.append(nc.dram_tensor(name, ins[name].shape, mybir.dt.from_np(ins[name].dtype),
                                   kind="ExternalInput").ap())
    args.append(nc.dram_tensor("out_rows", (OUT_ROWS, DIM), F32, kind="ExternalOutput").ap())
    decoder_layer(nc, *args)
    r = run_bass_kernel_spmd(nc, [ins], core_ids=[0])
    return r.results[0]["out_rows"][0:TOKENS].reshape(SEQS, LEN, DIM)
```
